# Optimizing a Trainium2 kernel written in Bass

```python
import numpy as np
import jax
import jax.numpy as jnp

def _softmax(x, axis=-1):
    return jax.nn.softmax(x, axis=axis)

def _gelu(x):
    return jax.nn.gelu(x, approximate=True)

def _silu(x):
    return jax.nn.silu(x)

def _sigmoid(x):
    return jax.nn.sigmoid(x)

def _layernorm(x, axis=-1, eps=1e-05):
    m = jnp.mean(x, axis=axis, keepdims=True)
    v = jnp.var(x, axis=axis, keepdims=True)
    return (x - m) / jnp.sqrt(v + eps)

def _scatter_add(tgt, idx, src, axis=0):
    return tgt.at[idx].add(src)

def _segment_sum(src, seg, n):
    return jax.ops.segment_sum(src, seg, n)
kernel_name = 'mk_sandwich_d2_jaxref_r8_d3a8d1'

def setup_inputs(seed: int=0):
    np.random.seed(seed)
    _w = jnp.asarray

    def _L0_attn_setup():
        import jax, jax.numpy as jnp
        import numpy as np
        DIM, HEADS, LAYERS, HID = (128, 16, 6, 512)
        PAST_CTX, MAX_PERIOD = (125, 10000.0)
        HEAD_DIM = DIM // HEADS

        def _ln(x, g, b, eps=1e-05):
            m = jnp.mean(x, axis=-1, keepdims=True)
            v = jnp.mean((x - m) ** 2, axis=-1, keepdims=True)
            return (x - m) * jax.lax.rsqrt(v + eps) * g + b

        def _forward(x, norm_in_g, norm_in_b, Wqkv, bqkv, Wo, bo, ln1_g, ln1_b, ln2_g, ln2_b, W1, b1, W2, b2):
            B, T, C = x.shape
            H = 1
            half = C // 2
            positions = jnp.arange(T, dtype=jnp.float32)[None, :, None]
            adim = jnp.arange(half, dtype=jnp.float32)[None, None, :]
            phase = positions / MAX_PERIOD ** (adim / (half - 1))
            pos_emb = jnp.concatenate([jnp.cos(phase), jnp.sin(phase)], axis=-1)
            x = _ln(x, norm_in_g, norm_in_b) + pos_emb
            q_pos = jnp.arange(H, T + H)[:, None]
            k_pos = jnp.arange(T + H)[None, :]
            delta = q_pos - k_pos
            valid = (delta >= 0) & (delta <= PAST_CTX)
            neg = jnp.finfo(x.dtype).min
            past = jnp.zeros((B, H, C), x.dtype)
            for l in range(LAYERS):
                keys = jnp.concatenate([past, x], axis=1)
                Wq, Wk, Wv = (Wqkv[l][:C], Wqkv[l][C:2 * C], Wqkv[l][2 * C:])
                bq, bk, bv = (bqkv[l][:C], bqkv[l][C:2 * C], bqkv[l][2 * C:])
                q = (x @ Wq.T + bq).reshape(B, T, HEADS, HEAD_DIM)
                k = (keys @ Wk.T + bk).reshape(B, T + H, HEADS, HEAD_DIM)
                v = (keys @ Wv.T + bv).reshape(B, T + H, HEADS, HEAD_DIM)
                scores = jnp.einsum('bqhd,bkhd->bhqk', q, k) / jnp.sqrt(jnp.asarray(HEAD_DIM, x.dtype))
                scores = jnp.where(valid[None, None], scores, neg)
                attn = jax.nn.softmax(scores, axis=-1)
                o = jnp.einsum('bhqk,bkhd->bqhd', attn, v).reshape(B, T, C)
                o = o @ Wo[l].T + bo[l]
                x = _ln(x + o, ln1_g[l], ln1_b[l])
                ff = jax.nn.gelu(x @ W1[l].T + b1[l], approximate=False) @ W2[l].T + b2[l]
                x = _ln(x + ff, ln2_g[l], ln2_b[l])
            return x
        key = jax.random.key(seed)
        ks = jax.random.split(key, 8)
        s = 0.02
        inp = {'x': jax.random.normal(ks[0], (2, 256, DIM), jnp.float32), 'norm_in_g': jnp.ones((DIM,), jnp.float32), 'norm_in_b': jnp.zeros((DIM,), jnp.float32), 'Wqkv': jax.random.normal(ks[1], (LAYERS, 3 * DIM, DIM), jnp.float32) * s, 'bqkv': jnp.zeros((LAYERS, 3 * DIM), jnp.float32), 'Wo': jax.random.normal(ks[2], (LAYERS, DIM, DIM), jnp.float32) * s, 'bo': jnp.zeros((LAYERS, DIM), jnp.float32), 'ln1_g': jnp.ones((LAYERS, DIM), jnp.float32), 'ln1_b': jnp.zeros((LAYERS, DIM), jnp.float32), 'ln2_g': jnp.ones((LAYERS, DIM), jnp.float32), 'ln2_b': jnp.zeros((LAYERS, DIM), jnp.float32), 'W1': jax.random.normal(ks[3], (LAYERS, HID, DIM), jnp.float32) * s, 'b1': jnp.zeros((LAYERS, HID), jnp.float32), 'W2': jax.random.normal(ks[4], (LAYERS, DIM, HID), jnp.float32) * s, 'b2': jnp.zeros((LAYERS, DIM), jnp.float32)}
        return inp
    _L0_attn_in = _L0_attn_setup()

    def _L0_ffn_setup():
        import jax, jax.numpy as jnp
        import numpy as np
        DIM = 128

        def _reference_tuple_inner(x, W_r, W_k, W_v, mu_r, mu_k):
            B, T, C = x.shape
            x_prev = jnp.concatenate([jnp.zeros((B, 1, C), x.dtype), x[:, :-1, :]], axis=1)
            xr = mu_r * x + (1.0 - mu_r) * x_prev
            xk = mu_k * x + (1.0 - mu_k) * x_prev
            r = jax.nn.sigmoid(jnp.einsum('btc,dc->btd', xr, W_r))
            k = jnp.einsum('btc,dc->btd', xk, W_k)
            k_act = jnp.square(jax.nn.relu(k))
            out = r * jnp.einsum('btc,dc->btd', k_act, W_v)
            new_state = x[:, -1, :]
            return (out, new_state)
        key = jax.random.key(seed)
        ks = jax.random.split(key, 6)
        B, T, C = (8, 256, DIM)
        x = jax.random.normal(ks[0], (B, T, C), dtype=jnp.float32)
        s = 1.0 / np.sqrt(C)
        W_r = jax.random.uniform(ks[1], (C, C), jnp.float32, -s, s)
        W_k = jax.random.uniform(ks[2], (C, C), jnp.float32, -s, s)
        W_v = jax.random.uniform(ks[3], (C, C), jnp.float32, -s, s)
        mu_r = jax.random.uniform(ks[4], (C,), jnp.float32)
        mu_k = jax.random.uniform(ks[5], (C,), jnp.float32)
        return {'x': x, 'W_r': W_r, 'W_k': W_k, 'W_v': W_v, 'mu_r': mu_r, 'mu_k': mu_k}
    _L0_ffn_in = _L0_ffn_setup()

    def _L1_attn_setup():
        import jax, jax.numpy as jnp
        import numpy as np
        import math
        PHI = (1.0 + math.sqrt(5.0)) / 2.0
        BASE_PHASES = [0.0, math.pi / 7, 2 * math.pi / 7, 3 * math.pi / 7, 4 * math.pi / 7, 5 * math.pi / 7, 6 * math.pi / 7]
        B, S, D, H = (4, 128, 128, 16)
        DH = D // H
        INITIAL_ACTIVE = 12
        BANDWIDTH_MAX = math.pi / 4
        EPS = 1e-06

        def _carrier_phases(n_heads):
            n_rungs = len(BASE_PHASES)
            raw_w = [1.0 / PHI ** i for i in range(n_rungs)]
            tot = sum(raw_w)
            alloc = [max(1, round(n_heads * w / tot)) for w in raw_w]
            while sum(alloc) > n_heads:
                alloc[alloc.index(max(alloc))] -= 1
            while sum(alloc) < n_heads:
                alloc[alloc.index(max(alloc))] += 1
            phases = []
            for r, count in enumerate(alloc):
                for j in range(count):
                    phases.append(BASE_PHASES[r] + 2 * math.pi / max(count, 1) * j)
            return np.asarray(phases, dtype=np.float32)

        def _forward(x, wq, wk, wv, wo, w_phase, carrier, lock, bandwidth, active_mask):
            b, s, d = x.shape

            def split_heads(t):
                return t.reshape(b, s, H, DH).transpose(0, 2, 1, 3)
            q = split_heads(x @ wq)
            k = split_heads(x @ wk)
            v = split_heads(x @ wv)
            ph = x @ w_phase
            phase = jnp.arctan2(ph[..., 0], ph[..., 1])
            dphi = phase[:, None, :] - carrier[None, :, None]
            window = jnp.exp((jnp.cos(dphi) - 1.0) / bandwidth[None, :, None])
            gate = lock[None, :, None] * window + (1.0 - lock[None, :, None])
            scores = jnp.einsum('bhqd,bhkd->bhqk', q, k) / math.sqrt(DH)
            scores = scores + jnp.log(gate + EPS)[:, :, None, :]
            causal = jnp.tril(jnp.ones((s, s), dtype=bool))
            scores = jnp.where(causal[None, None], scores, -jnp.inf)
            attn = jax.nn.softmax(scores, axis=-1)
            o = jnp.einsum('bhqk,bhkd->bhqd', attn, v)
            o = o * active_mask.astype(o.dtype)[None, :, None, None]
            y = o.transpose(0, 2, 1, 3).reshape(b, s, d) @ wo
            return y
        key = jax.random.key(seed)
        ks = jax.random.split(key, 8)
        sc = 1.0 / math.sqrt(D)
        x = jax.random.normal(ks[0], (B, S, D), dtype=jnp.float32)
        wq = jax.random.normal(ks[1], (D, D), dtype=jnp.float32) * sc
        wk = jax.random.normal(ks[2], (D, D), dtype=jnp.float32) * sc
        wv = jax.random.normal(ks[3], (D, D), dtype=jnp.float32) * sc
        wo = jax.random.normal(ks[4], (D, D), dtype=jnp.float32) * sc
        w_phase = jax.random.normal(ks[5], (D, 2), dtype=jnp.float32) * sc
        carrier = jnp.asarray(_carrier_phases(H))
        lock = jax.random.uniform(ks[6], (H,), dtype=jnp.float32)
        bandwidth = BANDWIDTH_MAX * (1.0 - lock) + 0.05
        active_mask = jnp.arange(H) < INITIAL_ACTIVE
        return {'x': x, 'wq': wq, 'wk': wk, 'wv': wv, 'wo': wo, 'w_phase': w_phase, 'carrier': carrier, 'lock': lock, 'bandwidth': bandwidth, 'active_mask': active_mask}
    _L1_attn_in = _L1_attn_setup()

    def _L1_ffn_setup():
        import jax, jax.numpy as jnp
        import numpy as np
        D_MODEL = 128
        D_FF = 512
        N_ZONES = 8
        TOP_K = 3
        ROUTER_H = 32
        BATCH = 16
        SEQ = 256
        key = jax.random.key(seed)
        ks = jax.random.split(key, 8)
        s = lambda *dims: 1.0 / np.sqrt(dims[-2] if len(dims) > 1 else dims[-1])
        x = jax.random.normal(ks[0], (BATCH, SEQ, D_MODEL), dtype=jnp.float32)
        W1 = jax.random.normal(ks[1], (D_MODEL, ROUTER_H), dtype=jnp.float32) / np.sqrt(D_MODEL)
        b1 = jnp.zeros((ROUTER_H,), dtype=jnp.float32)
        W2 = jax.random.normal(ks[2], (ROUTER_H, N_ZONES), dtype=jnp.float32) / np.sqrt(ROUTER_H)
        b2 = jnp.zeros((N_ZONES,), dtype=jnp.float32)
        Wa = jax.random.normal(ks[3], (N_ZONES, D_MODEL, D_FF), dtype=jnp.float32) / np.sqrt(D_MODEL)
        Wb = jax.random.normal(ks[4], (N_ZONES, D_FF, D_MODEL), dtype=jnp.float32) / np.sqrt(D_FF)
        return {'x': x, 'W1': W1, 'b1': b1, 'W2': W2, 'b2': b2, 'Wa': Wa, 'Wb': Wb}
    _L1_ffn_in = _L1_ffn_setup()
    _d = {'L0_attn_x': _L0_attn_in['x'], 'L0_attn_norm_in_g': _L0_attn_in['norm_in_g'], 'L0_attn_norm_in_b': _L0_attn_in['norm_in_b'], 'L0_attn_Wqkv': _L0_attn_in['Wqkv'], 'L0_attn_bqkv': _L0_attn_in['bqkv'], 'L0_attn_Wo': _L0_attn_in['Wo'], 'L0_attn_bo': _L0_attn_in['bo'], 'L0_attn_ln1_g': _L0_attn_in['ln1_g'], 'L0_attn_ln1_b': _L0_attn_in['ln1_b'], 'L0_attn_ln2_g': _L0_attn_in['ln2_g'], 'L0_attn_ln2_b': _L0_attn_in['ln2_b'], 'L0_attn_W1': _L0_attn_in['W1'], 'L0_attn_b1': _L0_attn_in['b1'], 'L0_attn_W2': _L0_attn_in['W2'], 'L0_attn_b2': _L0_attn_in['b2'], 'L0_ffn_W_r': _L0_ffn_in['W_r'], 'L0_ffn_W_k': _L0_ffn_in['W_k'], 'L0_ffn_W_v': _L0_ffn_in['W_v'], 'L0_ffn_mu_r': _L0_ffn_in['mu_r'], 'L0_ffn_mu_k': _L0_ffn_in['mu_k'], 'L1_attn_wq': _L1_attn_in['wq'], 'L1_attn_wk': _L1_attn_in['wk'], 'L1_attn_wv': _L1_attn_in['wv'], 'L1_attn_wo': _L1_attn_in['wo'], 'L1_attn_w_phase': _L1_attn_in['w_phase'], 'L1_attn_carrier': _L1_attn_in['carrier'], 'L1_attn_lock': _L1_attn_in['lock'], 'L1_attn_bandwidth': _L1_attn_in['bandwidth'], 'L1_attn_active_mask': _L1_attn_in['active_mask'], 'L1_ffn_W1': _L1_ffn_in['W1'], 'L1_ffn_b1': _L1_ffn_in['b1'], 'L1_ffn_W2': _L1_ffn_in['W2'], 'L1_ffn_b2': _L1_ffn_in['b2'], 'L1_ffn_Wa': _L1_ffn_in['Wa'], 'L1_ffn_Wb': _L1_ffn_in['Wb']}
    _x0 = _d['L0_attn_x']
    _d['L0_attn_x'] = jax.random.normal(jax.random.fold_in(jax.random.key(seed), 1), (4, 512, 128), dtype=_x0.dtype)
    del _x0
    return _d

def reference(L0_attn_x, L0_attn_norm_in_g, L0_attn_norm_in_b, L0_attn_Wqkv, L0_attn_bqkv, L0_attn_Wo, L0_attn_bo, L0_attn_ln1_g, L0_attn_ln1_b, L0_attn_ln2_g, L0_attn_ln2_b, L0_attn_W1, L0_attn_b1, L0_attn_W2, L0_attn_b2, L0_ffn_W_r, L0_ffn_W_k, L0_ffn_W_v, L0_ffn_mu_r, L0_ffn_mu_k, L1_attn_wq, L1_attn_wk, L1_attn_wv, L1_attn_wo, L1_attn_w_phase, L1_attn_carrier, L1_attn_lock, L1_attn_bandwidth, L1_attn_active_mask, L1_ffn_W1, L1_ffn_b1, L1_ffn_W2, L1_ffn_b2, L1_ffn_Wa, L1_ffn_Wb):

    def _L0_attn_ref(x, norm_in_g, norm_in_b, Wqkv, bqkv, Wo, bo, ln1_g, ln1_b, ln2_g, ln2_b, W1, b1, W2, b2):
        import jax, jax.numpy as jnp
        import numpy as np
        DIM, HEADS, LAYERS, HID = (128, 16, 6, 512)
        PAST_CTX, MAX_PERIOD = (125, 10000.0)
        HEAD_DIM = DIM // HEADS

        def _ln(x, g, b, eps=1e-05):
            m = jnp.mean(x, axis=-1, keepdims=True)
            v = jnp.mean((x - m) ** 2, axis=-1, keepdims=True)
            return (x - m) * jax.lax.rsqrt(v + eps) * g + b

        def _forward(x, norm_in_g, norm_in_b, Wqkv, bqkv, Wo, bo, ln1_g, ln1_b, ln2_g, ln2_b, W1, b1, W2, b2):
            B, T, C = x.shape
            H = 1
            half = C // 2
            positions = jnp.arange(T, dtype=jnp.float32)[None, :, None]
            adim = jnp.arange(half, dtype=jnp.float32)[None, None, :]
            phase = positions / MAX_PERIOD ** (adim / (half - 1))
            pos_emb = jnp.concatenate([jnp.cos(phase), jnp.sin(phase)], axis=-1)
            x = _ln(x, norm_in_g, norm_in_b) + pos_emb
            q_pos = jnp.arange(H, T + H)[:, None]
            k_pos = jnp.arange(T + H)[None, :]
            delta = q_pos - k_pos
            valid = (delta >= 0) & (delta <= PAST_CTX)
            neg = jnp.finfo(x.dtype).min
            past = jnp.zeros((B, H, C), x.dtype)
            for l in range(LAYERS):
                keys = jnp.concatenate([past, x], axis=1)
                Wq, Wk, Wv = (Wqkv[l][:C], Wqkv[l][C:2 * C], Wqkv[l][2 * C:])
                bq, bk, bv = (bqkv[l][:C], bqkv[l][C:2 * C], bqkv[l][2 * C:])
                q = (x @ Wq.T + bq).reshape(B, T, HEADS, HEAD_DIM)
                k = (keys @ Wk.T + bk).reshape(B, T + H, HEADS, HEAD_DIM)
                v = (keys @ Wv.T + bv).reshape(B, T + H, HEADS, HEAD_DIM)
                scores = jnp.einsum('bqhd,bkhd->bhqk', q, k) / jnp.sqrt(jnp.asarray(HEAD_DIM, x.dtype))
                scores = jnp.where(valid[None, None], scores, neg)
                attn = jax.nn.softmax(scores, axis=-1)
                o = jnp.einsum('bhqk,bkhd->bqhd', attn, v).reshape(B, T, C)
                o = o @ Wo[l].T + bo[l]
                x = _ln(x + o, ln1_g[l], ln1_b[l])
                ff = jax.nn.gelu(x @ W1[l].T + b1[l], approximate=False) @ W2[l].T + b2[l]
                x = _ln(x + ff, ln2_g[l], ln2_b[l])
            return x
        return _forward(x, norm_in_g, norm_in_b, Wqkv, bqkv, Wo, bo, ln1_g, ln1_b, ln2_g, ln2_b, W1, b1, W2, b2)

    def _L0_ffn_ref(x, W_r, W_k, W_v, mu_r, mu_k):
        import jax, jax.numpy as jnp
        import numpy as np
        DIM = 128

        def _reference_tuple_inner(x, W_r, W_k, W_v, mu_r, mu_k):
            B, T, C = x.shape
            x_prev = jnp.concatenate([jnp.zeros((B, 1, C), x.dtype), x[:, :-1, :]], axis=1)
            xr = mu_r * x + (1.0 - mu_r) * x_prev
            xk = mu_k * x + (1.0 - mu_k) * x_prev
            r = jax.nn.sigmoid(jnp.einsum('btc,dc->btd', xr, W_r))
            k = jnp.einsum('btc,dc->btd', xk, W_k)
            k_act = jnp.square(jax.nn.relu(k))
            out = r * jnp.einsum('btc,dc->btd', k_act, W_v)
            new_state = x[:, -1, :]
            return (out, new_state)
        return _reference_tuple_inner(x, W_r, W_k, W_v, mu_r, mu_k)[0]

    def _L1_attn_ref(x, wq, wk, wv, wo, w_phase, carrier, lock, bandwidth, active_mask):
        import jax, jax.numpy as jnp
        import numpy as np
        import math
        PHI = (1.0 + math.sqrt(5.0)) / 2.0
        BASE_PHASES = [0.0, math.pi / 7, 2 * math.pi / 7, 3 * math.pi / 7, 4 * math.pi / 7, 5 * math.pi / 7, 6 * math.pi / 7]
        B, S, D, H = (4, 128, 128, 16)
        DH = D // H
        INITIAL_ACTIVE = 12
        BANDWIDTH_MAX = math.pi / 4
        EPS = 1e-06

        def _carrier_phases(n_heads):
            n_rungs = len(BASE_PHASES)
            raw_w = [1.0 / PHI ** i for i in range(n_rungs)]
            tot = sum(raw_w)
            alloc = [max(1, round(n_heads * w / tot)) for w in raw_w]
            while sum(alloc) > n_heads:
                alloc[alloc.index(max(alloc))] -= 1
            while sum(alloc) < n_heads:
                alloc[alloc.index(max(alloc))] += 1
            phases = []
            for r, count in enumerate(alloc):
                for j in range(count):
                    phases.append(BASE_PHASES[r] + 2 * math.pi / max(count, 1) * j)
            return np.asarray(phases, dtype=np.float32)

        def _forward(x, wq, wk, wv, wo, w_phase, carrier, lock, bandwidth, active_mask):
            b, s, d = x.shape

            def split_heads(t):
                return t.reshape(b, s, H, DH).transpose(0, 2, 1, 3)
            q = split_heads(x @ wq)
            k = split_heads(x @ wk)
            v = split_heads(x @ wv)
            ph = x @ w_phase
            phase = jnp.arctan2(ph[..., 0], ph[..., 1])
            dphi = phase[:, None, :] - carrier[None, :, None]
            window = jnp.exp((jnp.cos(dphi) - 1.0) / bandwidth[None, :, None])
            gate = lock[None, :, None] * window + (1.0 - lock[None, :, None])
            scores = jnp.einsum('bhqd,bhkd->bhqk', q, k) / math.sqrt(DH)
            scores = scores + jnp.log(gate + EPS)[:, :, None, :]
            causal = jnp.tril(jnp.ones((s, s), dtype=bool))
            scores = jnp.where(causal[None, None], scores, -jnp.inf)
            attn = jax.nn.softmax(scores, axis=-1)
            o = jnp.einsum('bhqk,bhkd->bhqd', attn, v)
            o = o * active_mask.astype(o.dtype)[None, :, None, None]
            y = o.transpose(0, 2, 1, 3).reshape(b, s, d) @ wo
            return y
        return _forward(x, wq, wk, wv, wo, w_phase, carrier, lock, bandwidth, active_mask)

    def _L1_ffn_ref(x, W1, b1, W2, b2, Wa, Wb):
        import jax, jax.numpy as jnp
        import numpy as np
        D_MODEL = 128
        D_FF = 512
        N_ZONES = 8
        TOP_K = 3
        ROUTER_H = 32
        BATCH = 16
        SEQ = 256
        pooled = x.mean(axis=1)
        h = jnp.tanh(pooled @ W1 + b1)
        logits = h @ W2 + b2
        probs = jax.nn.softmax(logits, axis=-1)
        top_p, top_i = jax.lax.top_k(probs, TOP_K)
        top_w = top_p / top_p.sum(axis=-1, keepdims=True)
        onehot = jax.nn.one_hot(top_i, N_ZONES, dtype=x.dtype)
        w = jnp.einsum('bk,bke->be', top_w, onehot)
        zone_outputs = jnp.zeros_like(x)
        for e in range(N_ZONES):
            z = jax.nn.gelu(x @ Wa[e]) @ Wb[e]
            zone_outputs = zone_outputs + z * w[:, e, None, None]
        return x + zone_outputs
    x = L0_attn_x
    x = x + _layernorm(_L0_attn_ref(_layernorm(x, axis=-1), L0_attn_norm_in_g, L0_attn_norm_in_b, L0_attn_Wqkv, L0_attn_bqkv, L0_attn_Wo, L0_attn_bo, L0_attn_ln1_g, L0_attn_ln1_b, L0_attn_ln2_g, L0_attn_ln2_b, L0_attn_W1, L0_attn_b1, L0_attn_W2, L0_attn_b2), axis=-1)
    x = x + _layernorm(_L0_ffn_ref(_layernorm(x, axis=-1), L0_ffn_W_r, L0_ffn_W_k, L0_ffn_W_v, L0_ffn_mu_r, L0_ffn_mu_k), axis=-1)
    x = x + _layernorm(_L1_attn_ref(_layernorm(x, axis=-1), L1_attn_wq, L1_attn_wk, L1_attn_wv, L1_attn_wo, L1_attn_w_phase, L1_attn_carrier, L1_attn_lock, L1_attn_bandwidth, L1_attn_active_mask), axis=-1)
    x = x + _layernorm(_L1_ffn_ref(_layernorm(x, axis=-1), L1_ffn_W1, L1_ffn_b1, L1_ffn_W2, L1_ffn_b2, L1_ffn_Wa, L1_ffn_Wb), axis=-1)
    return x

_drawn_inputs = setup_inputs


def setup_inputs(seed=0):
    import zlib

    import numpy as np

    out = dict(_drawn_inputs(seed))
    spreads = {'L0_attn_norm_in_g': (1.0, 0.2),
     'L0_attn_norm_in_b': (0.0, 0.1),
     'L0_attn_bqkv': (0.0, 0.1),
     'L0_attn_bo': (0.0, 0.1),
     'L0_attn_ln1_g': (1.0, 0.2),
     'L0_attn_ln1_b': (0.0, 0.1),
     'L0_attn_ln2_g': (1.0, 0.2),
     'L0_attn_ln2_b': (0.0, 0.1),
     'L0_attn_b1': (0.0, 0.1),
     'L0_attn_b2': (0.0, 0.1),
     'L1_ffn_b1': (0.0, 0.1),
     'L1_ffn_b2': (0.0, 0.1)}
    factors = {}
    for name, (base, spread) in spreads.items():
        noise = np.random.default_rng([zlib.crc32(name.encode()), seed]).standard_normal(out[name].shape)
        drawn = base * np.exp(spread * noise) if base else spread * noise
        out[name] = jnp.asarray(drawn.astype(out[name].dtype))
    for name, factor in factors.items():
        out[name] = (out[name] * factor).astype(out[name].dtype)
    return out
```

```python
from contextlib import ExitStack

import concourse.bass as bass
from concourse import mybir

P = 128
BATCH, SEQ = 4, 512
TILES = SEQ // P
HEADS, HEAD = 16, 8
GROUPS = 4
LANES = HEADS // GROUPS
PAIRS = HEADS // 2
LAYERS, HIDDEN = 6, 512
CHUNKS = HIDDEN // P
EXPERTS, ROUTER, TOP = 8, 32, 3
WINDOW = 125
QROLES = (0, 0, 0, 1, 1, 2)
KROLES = (0, 1, 2, 0, 1, 0)
ROLES = len(QROLES)
ROWS = ROLES * HEAD
MAXROW = 2 * ROWS
PARTS = 2
CONTRACT = MAXROW + PARTS
VW = HEAD + 1
EPS = 1e-5
LOG_EPS = 1e-6
NEG = -1e30
LOWEST = -3.0e38
SCALE = float(1.0 / HEAD ** 0.5)

F32 = mybir.dt.float32
BF16 = mybir.dt.bfloat16
I32 = mybir.dt.int32
U32 = mybir.dt.uint32
ALU = mybir.AluOpType
ACT = mybir.ActivationFunctionType
AX = mybir.AxisListType

BQ, BK = 0, 1
BO, G1, H1, G2, H2, B2, B1 = range(7)
DCOLS = 6 + CHUNKS


class Windowed:

    keys = TILES + 1
    fills = [[(0, 0, 256, 0), (1, 128, 256, 256)], [(2, 256, 256, 0), (3, 384, 256, 256)]]
    pieces = [[(0, 0, 128, 0), (1, 0, 256, 128), (2, 128, 128, 384)],
              [(2, 256, 128, 0), (3, 256, 256, 128), (4, 384, 128, 384)]]
    widths = [512, 512]
    values = [(0, 0, 0, 128), (1, 128, 0, 256), (2, 384, 128, 256), (3, 640, 256, 256), (4, 896, 384, 128)]
    width = 1024
    split = 3


class Causal:

    keys = TILES
    fills = [[(0, 0, 128, 0), (1, 0, 256, 128)], [(2, 0, 384, 0)], [(3, 0, 512, 0)]]
    pieces = [[(0, 0, 512, 0)], [(1, 128, 384, 0)], [(2, 256, 256, 0), (3, 384, 128, 256)]]
    widths = [512, 384, 384]
    values = [(0, 0, 0, 512), (1, 512, 128, 384), (2, 896, 256, 256), (3, 1152, 384, 128)]
    width = 1280
    split = 1


class Unit:

    def __init__(self, n, parity, count, base=None):
        self.n = n
        self.par = parity
        self.there = not isinstance(n, int) or 0 <= n < count

    def value(self, per, k):
        return self.n * per + k


def needed(value):
    return not isinstance(value, int) or value > 0


def count(eng, value):
    return value if isinstance(value, int) else eng.to_reg(value)


def attention(nc, env, geo, full, units, loop):
    NF, NQ = len(geo.fills), len(geo.pieces)
    PF, PQ = NF * HEADS, NQ * HEADS
    COUNT = units
    KT = geo.keys
    KW = KT * P
    K0 = KW - SEQ
    ident, identb = env["ident"], env["identb"]
    state = env["state"]
    source, result = env["source"], env["result"]

    with ExitStack() as ctx:
        def sb(name, shape, dt=F32):
            return ctx.enter_context(nc.sbuf_tensor(f"{geo.__name__}_{name}", shape, dt))

        def ps(name):
            return ctx.enter_context(nc.psum_tensor(f"{geo.__name__}_{name}", [P, 512], F32))

        used = []
        def sem(name):
            used.append(ctx.enter_context(nc.semaphore(f"{geo.__name__}_{name}")))
            return used[-1]

        wqk = sb("wqk", [P, 2 * P])
        wv = sb("wv", [P, P])
        acols = sb("acols", [P, 2])
        bvb = sb("bvb", [P, P])
        wo = sb("wo", [P, P])
        xs = sb("xs", [P, SEQ])
        bqs = sb("bqs", [P, 1])
        zeros = sb("zeros", [P, P])
        qf, kf = sb("qf", [P, SEQ]), sb("kf", [P, KW])
        qparts, kparts = sb("qparts", [P, 3, SEQ], BF16), sb("kparts", [P, 3, KW], BF16)
        qpack = sb("qpack", [P, PAIRS, SEQ], BF16)
        kpack = sb("kpack", [P, PAIRS, KW], BF16)
        qz = sb("qz", [P, 2, HEADS, SEQ], BF16)
        keys = sb("keys", [P, 2, PAIRS, KW], BF16)
        VALS = KT * HEADS * VW
        vals = sb("vals", [P, 2, VALS + 32])
        junk = sb("junk", [P, 2 * TILES, 512], BF16)
        mx = sb("mx", [P, 2, HEADS, TILES])
        mparts = sb("mparts", [P, TILES, PARTS, HEADS // 2], BF16)
        mrows = sb("mrows", [PARTS * HEADS // 2, SEQ], BF16)
        probs = sb("probs", [P, 2, LANES, geo.width])
        sums = sb("sums", [P, GROUPS, SEQ])
        recips = sb("recips", [P, TILES, HEADS])
        otok = sb("otok", [P, TILES, P])
        ocat = sb("ocat", [P, SEQ])
        if full:
            w1, w2 = sb("w1", [P, HIDDEN]), sb("w2", [P, CHUNKS, P])
            dcols = sb("dcols", [P, DCOLS])
            y = sb("y", [P, 2, SEQ])
            stats, mv = sb("stats", [P, TILES, 6]), sb("mv", [P, TILES, 2])
            veps, rstd = sb("veps", [P, TILES]), sb("rstd", [P, TILES])
            ztok = sb("ztok", [P, TILES, P])
            xmid = sb("xmid", [P, SEQ])
            hid = env["rows"]

        st_ps = [ps("st0"), ps("st1")]
        fill_ps = [ps("fill0"), ps("fill1")]
        sum_ps = ps("sum")
        m0, m1, m2 = ps("m0"), ps("m1"), ps("m2")
        m2b = m2[:, :].bitcast(BF16)

        ready = sem("ready")
        wa_loaded, wv_loaded, wd_loaded = sem("wa_loaded"), sem("wv_loaded"), sem("wd_loaded")
        x_loaded = sem("x_loaded")
        v_proj, v_ready = sem("v_proj"), sem("v_ready")
        q_proj, k_proj = sem("q_proj"), sem("k_proj")
        q_bias, q_evac, k_evac = sem("q_bias"), sem("q_evac"), sem("k_evac")
        q_rest, k_rest, q_mid, k_mid = sem("q_rest"), sem("k_rest"), sem("q_mid"), sem("k_mid")
        q_lo, k_lo = sem("q_lo"), sem("k_lo")
        q_packed, k_packed, heads_loaded = sem("q_packed"), sem("k_packed"), sem("heads_loaded")
        filled, maxed = sem("filled"), sem("maxed")
        part_step, mparts_ready = sem("part_step"), sem("mparts_ready")
        mparts_turned, mrows_ready, max_loaded = sem("mparts_turned"), sem("mrows_ready"), sem("max_loaded")
        st_filled, exped, masked = sem("st_filled"), sem("exped"), sem("masked")
        summed, sums_ready = sem("summed"), sem("sums_ready")
        sums_turned, recip_ready, otok_ready = sem("sums_turned"), sem("recip_ready"), sem("otok_ready")
        otok_turned, ocat_ready, out_proj, y_ready = (sem("otok_turned"), sem("ocat_ready"), sem("out_proj"),
                                                      sem("y_ready"))
        y_turned, stats_ready, mv_ready = sem("y_turned"), sem("stats_ready"), sem("mv_ready")
        veps_ready, rstd_ready, z_ready = sem("veps_ready"), sem("rstd_ready"), sem("z_ready")
        z_turned, ln_ready = sem("z_turned"), sem("ln_ready")
        hid_proj, hid_ready, ffn_proj = sem("hid_proj"), sem("hid_ready"), sem("ffn_proj")

        WA, WV, WD = (2, 2, 4) if full else (1, 1, 1)
        READY = 6
        NLN = 2 if full else 1
        MASKS = 2 * LANES + 1 if full else 2 * LANES
        QD = KD = 16 * ROLES

        def vhead(par, kt, h):
            at = (kt * HEADS + h) * VW
            return vals[:, par, at:at + 32]

        def vview(par):
            return vals[:, par, 0:VALS].rearrange("p (t h c) -> p t h c", h=HEADS, c=VW)

        def layer(u):
            return u.n // BATCH

        def x_of(u):
            if isinstance(u.n, int):
                return source[:, u.n % BATCH, :]
            return source[:, bass.ds(u.n % BATCH, 1), :].rearrange("p a t -> p (a t)")

        def out_of(u):
            if isinstance(u.n, int):
                return result[:, u.n % BATCH, :]
            return result[:, bass.ds(u.n % BATCH, 1), :].rearrange("p a t -> p (a t)")

        def steps(eng, body):
            if loop is None:
                for k in range(units + 3):
                    body(k, k % 2)
                return
            for k in range(loop[0]):
                body(k, k % 2)
            with eng.Fori(loop[0], loop[1], 2) as k:
                body(k, 0)
                body(k + 1, 1)
            for k in range(loop[1], units + 3):
                body(k, k % 2)

        def stage_units(k, par):
            return [Unit(k - s, (par - s) % 2, COUNT) for s in range(4)]

        def max_unit(s, b, c):
            return (b, s - 3) if s >= 3 else (c, HEADS - 3 + s)

        def sum_unit(s, c, d):
            return {5: (c, 0), 9: (c, 1), 13: (c, 2), 1: (d, 3)}.get(s)

        ctx.callback(lambda: clear(nc, used))
        block = ctx.enter_context(nc.Block())

        @block.tensor
        def _(pe):
            def scores_t(c, h, q):
                at = h * NQ + q
                if needed(c.value(PQ, at - 1)):
                    pe.wait_ge(exped, c.value(PQ, at - 1))
                if at == 0:
                    pe.wait_ge(heads_loaded, c.value(48, 48))
                    pe.wait_ge(max_loaded, c.value(32, 16))
                if h == HEADS // 2 and q == 0:
                    pe.wait_ge(max_loaded, c.value(32, 32))
                for n, (kt, q0, nq, col) in enumerate(geo.pieces[q]):
                    mm = pe.matmul(st_ps[at % 2][:, col:col + nq], keys[0:CONTRACT, c.par, h // 2, kt * P:kt * P + P],
                                   qz[0:CONTRACT, c.par, h, q0:q0 + nq], start=True, stop=True)
                mm.then_inc(st_filled, 1)

            def scores(u, h, f):
                at = h * NF + f
                if needed(u.value(PF, at - 1)):
                    pe.wait_ge(maxed, u.value(PF, at - 1))
                if at == 0:
                    pe.wait_ge(heads_loaded, u.value(48, 48))
                for i, k0, nk, col in geo.fills[f]:
                    mm = pe.matmul(fill_ps[at % 2][:, col:col + nk], qz[0:MAXROW, u.par, h, i * P:i * P + P],
                                   keys[0:MAXROW, u.par, h // 2, k0:k0 + nk], start=True, stop=True)
                mm.then_inc(filled, 1)

            def weighted(u, g, turn):
                if turn == 0:
                    pe.wait_ge(masked, u.value(GROUPS * MASKS, MASKS * (g + 1)))
                    pe.wait_ge(v_ready, u.value(1, 1))
                    if needed(u.value(GROUPS, g)):
                        pe.wait_ge(sums_ready, u.value(GROUPS, g))
                for n, (kt, col, q0, nq) in enumerate(geo.values):
                    if (n >= geo.split) != (turn == 1):
                        continue
                    for j in range(LANES):
                        mm = pe.matmul(sum_ps[32 * j:32 * j + 32, q0:q0 + nq], vhead(u.par, kt, LANES * g + j),
                                       probs[:, g % 2, j, col:col + nq], start=(n == 0),
                                       stop=True, skip_group_check=True)
                if turn == 1:
                    mm.then_inc(summed, 1)

            def turn4(bank, src, done):
                for i in range(TILES):
                    mm = pe.transpose(bank[:, i * P:(i + 1) * P], src(i), ident[:, :])
                mm.then_inc(done, 1)

            def project_v(b):
                pe.wait_ge(wv_loaded, (layer(b) + 1) * 16 * WV)
                pe.wait_ge(x_loaded, b.value(16, 16))
                if needed(b.value(2, -1)):
                    pe.wait_ge(mrows_ready, b.value(2, -1))
                if full:
                    if needed((b.n - 2) * 2):
                        pe.wait_ge(y_ready, (b.n - 2) * 2)
                for i in range(TILES):
                    mm = pe.matmul(m2[:, i * P:(i + 1) * P], xs[:, i * P:(i + 1) * P], wv[:, :], start=True, stop=True)
                mm.then_inc(v_proj, 1)

            def turn_parts(u, half, b, d):
                pe.wait_ge(mparts_ready, u.value(2, half + 1))
                if needed(u.value(2, half)):
                    pe.wait_ge(mrows_ready, u.value(2, half))
                if b.there:
                    pe.wait_ge(v_ready, b.value(1, 1))
                if full and not half and d.there:
                    pe.wait_ge(y_ready, d.value(2, 2))
                for i in range(TILES):
                    mm = pe.transpose(m2b[0:PARTS * HEADS // 2, i * P:(i + 1) * P],
                                      mparts[:, i, :, :].rearrange("p a h -> p (a h)"), identb[:, :])
                mm.then_inc(mparts_turned, 1)

            def project_qk(a, d, which):
                if which == 0:
                    pe.wait_ge(wa_loaded, (layer(a) + 1) * 16 * WA)
                    pe.wait_ge(x_loaded, a.value(16, 16))
                    if needed(a.value(2, 0)):
                        pe.wait_ge(k_evac, a.value(2, 0))
                    if d.there:
                        pe.wait_ge(y_ready, d.value(NLN, 1))
                    if full and d.there:
                        if needed(d.value(2, 0)):
                            pe.wait_ge(ln_ready, d.value(2, 0))
                else:
                    pe.wait_ge(q_evac, a.value(2, 2))
                pe.matmul(m1[:, :], wqk[:, which * P:(which + 1) * P], xs[:, :], start=True, stop=True
                          ).then_inc(q_proj if which == 0 else k_proj, 1)

            def turn_sums(d, a, i):
                bank = m1 if i % 2 else m0
                pe.wait_ge(sums_ready, d.value(GROUPS, GROUPS))
                if i == 0 and full:
                    if needed(d.value(2, 0)):
                        pe.wait_ge(z_ready, d.value(2, 0))
                if i == 0 and not full:
                    if needed(d.value(1, 0)):
                        pe.wait_ge(ocat_ready, d.value(1, 0))
                if i == 1:
                    pe.wait_ge(k_evac, d.n * 2 + 6 if not isinstance(d.n, int) else min((d.n + 3), COUNT) * 2)
                    if full:
                        if needed(d.value(2, 0)):
                            pe.wait_ge(ln_ready, d.value(2, 0))
                    else:
                        if needed(d.value(1, 0)):
                            pe.wait_ge(y_ready, d.value(1, 0))
                if i >= 2:
                    if needed(d.value(TILES, i - 1)):
                        pe.wait_ge(otok_ready, d.value(TILES, i - 1))
                for g in range(GROUPS):
                    mm = pe.transpose(bank[:, g * P:(g + 1) * P], sums[:, g, i * P:(i + 1) * P], ident[:, :])
                mm.then_inc(sums_turned, 1)

            def turn_otok(d):
                pe.wait_ge(otok_ready, d.value(TILES, TILES))
                turn4(m0, lambda i: otok[:, i, :], otok_turned)

            def project_out(d):
                pe.wait_ge(ocat_ready, d.value(1, 1))
                pe.wait_ge(wd_loaded, (layer(d) + 1) * 16 * WD)
                pe.matmul(m1[:, :], wo[:, :], ocat[:, :], start=True, stop=True).then_inc(out_proj, 1)

            def turn_y(d, ln):
                pe.wait_ge(y_ready, d.value(2, ln + 1))
                if ln == 0:
                    pe.wait_ge(ocat_ready, d.value(1, 1))
                else:
                    pe.wait_ge(hid_ready, d.value(CHUNKS, CHUNKS))
                turn4(m0, lambda i: y[:, ln, i * P:(i + 1) * P], y_turned)

            def turn_z(d, ln):
                bank = m0 if ln == 0 else m1
                pe.wait_ge(z_ready, d.value(2, ln + 1))
                if ln == 1:
                    pe.wait_ge(hid_ready, d.value(CHUNKS, CHUNKS))
                turn4(bank, lambda i: ztok[:, i, :], z_turned)

            def hidden(d, a, f):
                if f == 0:
                    pe.wait_ge(ln_ready, d.value(2, 1))
                if f == 1 and a.there:
                    pe.wait_ge(k_evac, a.value(2, 2))
                if f >= 2:
                    pe.wait_ge(hid_ready, d.value(CHUNKS, f - 1))
                pe.matmul((m1 if f % 2 else m0)[:, :], w1[:, f * P:(f + 1) * P], xmid[:, :], start=True, stop=True
                          ).then_inc(hid_proj, 1)

            def second(d, c, b, f):
                if f == 0 and c.there:
                    pe.wait_ge(mrows_ready, c.value(2, 2))
                if f == 0 and b.there:
                    pe.wait_ge(v_ready, b.value(1, 1))
                pe.wait_ge(hid_ready, d.value(CHUNKS, f + 1))
                mm = pe.matmul(m2[:, :], w2[:, f, :], hid[:, f, :], start=(f == 0), stop=(f == CHUNKS - 1))
                if f == CHUNKS - 1:
                    mm.then_inc(ffn_proj, 1)

            pe.wait_ge(ready, READY)

            def middle(s, a, b, c, d):
                who = sum_unit(s, c, d)
                if who and who[0].there:
                    weighted(*who, 0)
                if s == 10 and d.there and full:
                    hidden(d, a, 0)
                if s == 11 and d.there and full:
                    hidden(d, a, 2)

            def end(s, a, b, c, d):
                who = sum_unit(s, c, d)
                if who and who[0].there:
                    weighted(*who, 1)
                if s == 2 and b.there:
                    project_v(b)
                if s == 3 and d.there:
                    turn_sums(d, a, 0)
                    turn_sums(d, a, 1)
                if s == 4:
                    if d.there:
                        turn_sums(d, a, 2)
                        turn_sums(d, a, 3)
                    if c.there:
                        turn_parts(c, 1, b, d)
                if s == 5 and d.there:
                    turn_otok(d)
                if s == 6 and d.there:
                    project_out(d)
                if s == 7 and d.there and full:
                    turn_y(d, 0)
                if s == 8 and a.there:
                    project_qk(a, d, 0)
                if s == 9:
                    if d.there and full:
                        turn_z(d, 0)
                    if a.there:
                        project_qk(a, d, 1)
                if s == 10 and d.there and full:
                    hidden(d, a, 1)
                if s == 11 and d.there and full:
                    hidden(d, a, 3)
                    for f in range(CHUNKS):
                        second(d, c, b, f)
                if s == 12 and d.there and full:
                    turn_y(d, 1)
                if s == 13 and b.there:
                    turn_parts(b, 0, b, d)
                if s == 14 and d.there and full:
                    turn_z(d, 1)

            def step(k, par):
                a, b, c, d = stage_units(k, par)
                for s in range(HEADS):
                    u, h = max_unit(s, b, c)
                    late = full and s == 12
                    if c.there and not late:
                        scores_t(c, s, 0)
                    if u.there:
                        scores(u, h, 0)
                    middle(s, a, b, c, d)
                    if c.there and not late:
                        scores_t(c, s, 1)
                    if u.there:
                        scores(u, h, 1)
                    for q in range(2, NQ):
                        if c.there:
                            scores_t(c, s, q)
                        if u.there:
                            scores(u, h, q)
                    end(s, a, b, c, d)
                    if c.there and late:
                        scores_t(c, s, 0)
                        scores_t(c, s, 1)

            steps(pe, step)

        @block.scalar
        def _(act):
            def exponent(c, h, q):
                at = h * NQ + q
                g, j = divmod(h, LANES)
                act.wait_ge(st_filled, c.value(PQ, at + 1))
                if j == 0 and q == 0:
                    if needed(c.value(GROUPS, g - 1)):
                        act.wait_ge(summed, c.value(GROUPS, g - 1))
                w, col = geo.widths[q], sum(geo.widths[:q])
                act.activation(probs[:, g % 2, j, col:col + w], st_ps[at % 2][:, 0:w], ACT.Exp).then_inc(exped, 1)

            def copy_sums(u, g):
                act.wait_ge(summed, u.value(GROUPS, g + 1))
                if needed(u.value(TILES, 0)):
                    act.wait_ge(sums_turned, u.value(TILES, 0))
                act.copy(sums[:, g, :], sum_ps[:, :]).then_inc(sums_ready, 1)

            def evacuate_q(a):
                act.wait_ge(q_proj, a.value(1, 1))
                act.wait_ge(wa_loaded, (layer(a) + 1) * 16 * WA)
                if full:
                    act.mul(bqs[:, :], acols[:, BQ:BQ + 1], SCALE).then_inc(q_bias, 1)
                    act.wait_ge(q_bias, a.value(1, 1))
                if needed(a.value(QD, 0)):
                    act.wait_ge(q_packed, a.value(QD, 0))
                bias = bqs[:, 0:1] if full else 0.0
                act.activation(qf[:, :], m1[:, :], ACT.Identity, bias=bias, scale=SCALE).then_inc(q_evac, 1)
                act.activation(qparts[:, 0, :], m1[:, :], ACT.Identity, bias=bias, scale=SCALE).then_inc(q_evac, 1)

            def evacuate_k(a):
                bias = acols[:, BK:BK + 1] if full else 0.0
                act.wait_ge(k_proj, a.value(1, 1))
                if needed(a.value(KD, 0)):
                    act.wait_ge(k_packed, a.value(KD, 0))
                if full:
                    act.activation(kf[:, 0:K0], zeros[:, 0:K0], ACT.Identity, bias=bias)
                    act.activation(kparts[:, 0, 0:K0], zeros[:, 0:K0], ACT.Identity, bias=bias)
                act.activation(kf[:, K0:KW], m1[:, :], ACT.Identity, bias=bias).then_inc(k_evac, 1)
                act.activation(kparts[:, 0, K0:KW], m1[:, :], ACT.Identity, bias=bias).then_inc(k_evac, 1)

            def copy_parts(u, half):
                act.wait_ge(mparts_turned, u.value(2, half + 1))
                if needed(u.value(32, 16 * half)):
                    act.wait_ge(max_loaded, u.value(32, 16 * half))
                act.copy(mrows[:, :], m2b[0:PARTS * HEADS // 2, 0:SEQ]).then_inc(mrows_ready, 1)

            def copy_heads(d):
                act.wait_ge(otok_turned, d.value(1, 1))
                if needed(d.value(1, 0)):
                    act.wait_ge(out_proj, d.value(1, 0))
                act.copy(ocat[:, :], m0[:, :]).then_inc(ocat_ready, 1)

            def copy_out(d):
                act.wait_ge(out_proj, d.value(1, 1))
                act.copy(out_of(d), m1[:, :]).then_inc(y_ready, 1)

            def norm_out(d, ln):
                act.wait_ge(z_turned, d.value(2, ln + 1))
                gain, shift = (G1, H1) if ln == 0 else (G2, H2)
                if ln == 0:
                    if needed(d.value(2, 0)):
                        act.wait_ge(y_ready, d.value(2, 0))
                    if needed(d.value(CHUNKS, 0)):
                        act.wait_ge(hid_proj, d.value(CHUNKS, 0))
                    act.wait_ge(wd_loaded, (layer(d) + 1) * 16 * WD)
                act.activation(xmid[:, :] if ln == 0 else out_of(d), (m0 if ln == 0 else m1)[:, :], ACT.Identity,
                               bias=dcols[:, shift:shift + 1], scale=dcols[:, gain:gain + 1]).then_inc(ln_ready, 1)

            def gelu(d):
                if needed(d.value(1, 0)):
                    act.wait_ge(ffn_proj, d.value(1, 0))
                for f in range(CHUNKS):
                    act.wait_ge(hid_proj, d.value(CHUNKS, f + 1))
                    act.activation(hid[:, f, :], (m1 if f % 2 else m0)[:, :], ACT.Gelu,
                                   bias=dcols[:, B1 + f:B1 + f + 1]).then_inc(hid_ready, 1)

            act.wait_ge(ready, READY)

            def step(k, par):
                a, b, c, d = stage_units(k, par)
                for s in range(HEADS):
                    if c.there:
                        for q in range(NQ):
                            exponent(c, s, q)
                    who = sum_unit(s, c, d)
                    if who and who[0].there:
                        copy_sums(*who)
                    if s == 4 and c.there:
                        copy_parts(c, 1)
                    if s == 5 and d.there:
                        copy_heads(d)
                    if s == 6 and d.there and not full:
                        copy_out(d)
                    if s == 8 and a.there:
                        evacuate_q(a)
                    if s == 9:
                        if d.there and full:
                            norm_out(d, 0)
                        if a.there:
                            evacuate_k(a)
                    if s == 10 and d.there and full:
                        gelu(d)
                    if s == 13 and b.there:
                        copy_parts(b, 0)
                    if s == 14 and d.there and full:
                        norm_out(d, 1)

            steps(act, step)

        @block.vector
        def _(dve):
            def maxima(u, h, f):
                at = count(dve, u.value(PF, h * NF + f + 1))
                dve.wait_ge(ready, READY)
                dve.wait_ge(filled, at)
                for n, (i, k0, nk, col) in enumerate(geo.fills[f]):
                    tt = dve.tensor_tensor_reduce(junk[:, h % 2 * TILES + i, 0:nk], fill_ps[(h * NF + f) % 2][:, col:col + nk],
                                                  env["mask"][:, env["mask"].shape[1] - nk:], 1.0, LOWEST,
                                                  ALU.add, ALU.max, mx[:, u.par, h, i:i + 1])
                tt.then_inc(maxed, 1)

            def parts(u, half):
                H = HEADS // 2
                top = mx[:, u.par, half * H:(half + 1) * H, :].rearrange("p h i -> p i h")
                dve.wait_ge(maxed, u.value(PF, NF * H * (half + 1)))
                if needed(u.value(2, half)):
                    dve.wait_ge(mparts_turned, u.value(2, half))
                dve.tensor_scalar(mparts[:, :, 0, :], top, -1.0, None, ALU.mult).then_inc(part_step, 1)
                dve.wait_ge(part_step, u.value(2, half + 1))
                dve.scalar_tensor_tensor(out=mparts[:, :, 1, :], in0=top, scalar=-1.0, in1=mparts[:, :, 0, :],
                                         op0=ALU.mult, op1=ALU.subtract).then_inc(mparts_ready, 1)

            def take_values(b):
                dve.wait_ge(v_proj, b.value(1, 1))
                dve.wait_ge(wv_loaded, (layer(b) + 1) * 16 * WV)
                if needed((b.n - 1) * GROUPS):
                    dve.wait_ge(summed, (b.n - 1) * GROUPS)
                v = vview(b.par)
                p4 = m2[:, :].rearrange("p (t h c) -> p t h c", h=HEADS, c=HEAD)
                if full:
                    dve.tensor_scalar(v[:, 0, :, 0:HEAD], bvb[:, :].rearrange("p (h c) -> p h c", c=HEAD),
                                      env["last_row"][:, 0:1], None, ALU.mult)
                    bias = bvb[:, :].rearrange("p (o h c) -> p o h c", o=1, c=HEAD).to_broadcast([P, TILES, HEADS, HEAD])
                    dve.tensor_tensor(v[:, 1:, :, 0:HEAD], p4, bias, ALU.add).then_inc(v_ready, 1)
                else:
                    g = env["gate"][:, (b.n % BATCH) * TILES:(b.n % BATCH + 1) * TILES, :]
                    dve.tensor_copy(v[:, :, :, HEAD:VW], g.unsqueeze(3))
                    dve.tensor_tensor(v[:, :, :, 0:HEAD], p4, g.unsqueeze(3).to_broadcast([P, TILES, HEADS, HEAD]),
                                      ALU.mult).then_inc(v_ready, 1)

            def normalise_heads(d, i):
                bank = (m1 if i % 2 else m0)[:, :].rearrange("p (h c) -> p h c", c=32)
                dve.wait_ge(sums_turned, d.value(TILES, i + 1))
                if i == 0:
                    if needed(d.value(1, 0)):
                        dve.wait_ge(otok_turned, d.value(1, 0))
                dve.reciprocal(recips[:, i, :], bank[:, :, HEAD:HEAD + 1].rearrange("p h c -> p (h c)")
                               ).then_inc(recip_ready, 1)
                per = TILES * (1 if full else 2)
                if not full:
                    dve.wait_ge(recip_ready, d.value(per, 2 * i + 1))
                    dve.tensor_tensor(recips[:, i, :], recips[:, i, :], env["active"][:, :], ALU.mult
                                      ).then_inc(recip_ready, 1)
                dve.wait_ge(recip_ready, d.value(per, (i + 1) * (1 if full else 2)))
                dve.tensor_tensor(otok[:, i, :].rearrange("p (h c) -> p h c", c=HEAD), bank[:, :, 0:HEAD],
                                  recips[:, i, :].unsqueeze(2).to_broadcast([P, HEADS, HEAD]), ALU.mult
                                  ).then_inc(otok_ready, 1)

            def residual(d, ln):
                if ln == 0:
                    dve.wait_ge(out_proj, d.value(1, 1))
                    dve.wait_ge(wd_loaded, (layer(d) + 1) * 16 * WD)
                    if needed(d.value(2, 0)):
                        dve.wait_ge(y_turned, d.value(2, 0))
                    dve.scalar_tensor_tensor(out=y[:, 0, :], in0=m1[:, :], scalar=dcols[:, BO:BO + 1], in1=out_of(d),
                                             op0=ALU.add, op1=ALU.add).then_inc(y_ready, 1)
                else:
                    dve.wait_ge(ffn_proj, d.value(1, 1))
                    dve.scalar_tensor_tensor(out=y[:, 1, :], in0=m2[:, :], scalar=dcols[:, B2:B2 + 1], in1=xmid[:, :],
                                             op0=ALU.add, op1=ALU.add).then_inc(y_ready, 1)

            def normalise(d, ln):
                dve.wait_ge(y_turned, d.value(2, ln + 1))
                for i in range(TILES):
                    bn = dve.bn_stats(stats[:, i, :], m0[:, i * P:(i + 1) * P])
                bn.then_inc(stats_ready, 1)
                at = count(dve, d.value(2, ln + 1))
                dve.wait_ge(ready, READY)
                dve.wait_ge(stats_ready, at)
                if needed(d.value(2, ln)):
                    dve.wait_ge(veps_ready, d.value(2, ln))
                for i in range(TILES):
                    bn = dve.bn_aggr(mv[:, i, :], stats[:, i, :])
                bn.then_inc(mv_ready, 1)

            def scale_rows(d, ln):
                dve.wait_ge(rstd_ready, d.value(2, ln + 1))
                if needed(d.value(2, ln)):
                    dve.wait_ge(z_turned, d.value(2, ln))
                for i in range(TILES):
                    z = dve.tensor_scalar(ztok[:, i, :], m0[:, i * P:(i + 1) * P], mv[:, i, 0:1], rstd[:, i:i + 1],
                                          ALU.subtract, ALU.mult)
                z.then_inc(z_ready, 1)

            def rests(a, which):
                if which == 0:
                    dve.wait_ge(q_evac, a.value(2, 2))
                    dve.tensor_tensor(qf[:, :], qf[:, :], qparts[:, 0, :], ALU.subtract).then_inc(q_rest, 1)
                else:
                    dve.wait_ge(k_evac, a.value(2, 2))
                    dve.tensor_tensor(kf[:, :], kf[:, :], kparts[:, 0, :], ALU.subtract).then_inc(k_rest, 1)

            dve.memset(zeros[:, :], 0.0).then_inc(ready, 1)
            dve.memset(qz[:, 0, :, :], 0.0).then_inc(ready, 1)
            dve.memset(qz[:, 1, :, :], 0.0).then_inc(ready, 1)
            dve.memset(vals[:, :, :], 0.0).then_inc(ready, 1)
            dve.wait_ge(ready, READY - 1)
            if full:
                for par in range(2):
                    dve.memset(vview(par)[:, 1:, :, HEAD:VW], 1.0)
                    one = dve.tensor_scalar(vview(par)[:, 0, :, HEAD:VW], vview(par)[:, 0, :, HEAD:VW],
                                            env["last_row"][:, 0:1], None, ALU.add)
                one.then_inc(ready, 1)
            else:
                dve.memset(zeros[:, 0:1], 0.0).then_inc(ready, 1)
            dve.wait_ge(ready, READY)

            def step(k, par):
                a, b, c, d = stage_units(k, par)
                for s in range(HEADS):
                    u, h = max_unit(s, b, c)
                    if u.there:
                        for f in range(NF):
                            maxima(u, h, f)
                    if s == 2:
                        if c.there:
                            parts(c, 1)
                        if b.there:
                            take_values(b)
                    if s == 3 and d.there:
                        normalise_heads(d, 0)
                        normalise_heads(d, 1)
                    if s == 4 and d.there:
                        normalise_heads(d, 2)
                        normalise_heads(d, 3)
                    if s == 6 and d.there and full:
                        residual(d, 0)
                    if s == 7 and d.there and full:
                        normalise(d, 0)
                    if s == 8:
                        if d.there and full:
                            scale_rows(d, 0)
                        if a.there:
                            rests(a, 0)
                    if s == 9 and a.there:
                        rests(a, 1)
                    if s == 11 and b.there:
                        parts(b, 0)
                    if s == 11 and d.there and full:
                        residual(d, 1)
                    if s == 12 and d.there and full:
                        normalise(d, 1)
                    if s == 13 and d.there and full:
                        scale_rows(d, 1)

            steps(dve, step)

        @block.gpsimd
        def _(pool):
            def mask(c, h):
                g, j = divmod(h, LANES)
                at = count(pool, c.value(PQ, NQ * (h + 1)))
                pool.wait_ge(ready, READY)
                pool.wait_ge(exped, at)
                row = probs[:, g % 2, j, :]
                if full:
                    both = row.rearrange("p (t two q) -> p two t q", two=2, q=P)
                    pool.affine_select(out=both[:, 0, :, :], in_=both[:, 0, :, :], compare_op=ALU.is_ge, fill=0.0,
                                       base=WINDOW - P, pattern=[[0, TILES], [-1, P]], channel_multiplier=1
                                       ).then_inc(masked, 1)
                    pool.affine_select(out=both[:, 1, :, :], in_=both[:, 1, :, :], compare_op=ALU.is_ge, fill=0.0,
                                       base=0, pattern=[[0, TILES], [1, P]], channel_multiplier=-1).then_inc(masked, 1)
                else:
                    for col, last in ((0, False), (512, True), (896, False), (1152, True)):
                        own = row[:, col:col + P]
                        sel = pool.affine_select(out=own, in_=own, compare_op=ALU.is_ge, fill=0.0, base=0,
                                                 pattern=[[1, P]], channel_multiplier=-1)
                        if last:
                            sel.then_inc(masked, 1)

            def mask_first(c, g):
                at = count(pool, c.value(GROUPS * MASKS, g * MASKS + 2 * LANES))
                pool.wait_ge(ready, READY)
                pool.wait_ge(masked, at)
                first = WINDOW + 1
                late = probs[:, g % 2, :, :].rearrange("p j (t two q) -> p j t two q", two=2, q=P)[:, :, :, 1, first:]
                pool.affine_select(out=late, in_=late, compare_op=ALU.is_ge, fill=0.0, base=WINDOW - first,
                                   pattern=[[0, LANES], [0, TILES], [-1, P - first]], channel_multiplier=1
                                   ).then_inc(masked, 1)

            def root(d, ln):
                at = count(pool, d.value(2, ln + 1))
                pool.wait_ge(ready, READY)
                pool.wait_ge(mv_ready, at)
                if needed(d.value(2, ln)):
                    pool.wait_ge(z_ready, d.value(2, ln))
                pool.tensor_scalar(veps[:, :], mv[:, :, 1], EPS, None, ALU.add).then_inc(veps_ready, 1)
                pool.wait_ge(veps_ready, d.value(2, ln + 1))
                pool.tensor_tensor(rstd[:, :], veps[:, :], env["minus_half"][:, 0:TILES], ALU.pow
                                   ).then_inc(rstd_ready, 1)

            def lower_parts(a, rest, parts, rest_ready, mid, low):
                at = count(pool, a.value(1, 1))
                pool.wait_ge(ready, READY)
                pool.wait_ge(rest_ready, at)
                pool.tensor_copy(parts[:, 1, :], rest[:, :]).then_inc(mid, 1)
                at = count(pool, a.value(1, 1))
                pool.wait_ge(ready, READY)
                pool.wait_ge(mid, at)
                pool.tensor_tensor(parts[:, 2, :], rest[:, :], parts[:, 1, :], ALU.subtract).then_inc(low, 1)

            pool.memset(keys[MAXROW:CONTRACT, :, :, :], 1.0).then_inc(ready, 1)

            def step(k, par):
                a, b, c, d = stage_units(k, par)
                for s in range(HEADS):
                    if c.there:
                        mask(c, s)
                        if full and s % LANES == LANES - 1:
                            mask_first(c, s // LANES)
                    if s == 7 and d.there and full:
                        root(d, 0)
                    if s == 9 and a.there:
                        lower_parts(a, qf, qparts, q_rest, q_mid, q_lo)
                    if s == 10 and a.there:
                        lower_parts(a, kf, kparts, k_rest, k_mid, k_lo)
                    if s == 12 and d.there and full:
                        root(d, 1)

            steps(pool, step)

        @block.sync
        def _(sp):
            w = env["weights"]

            def row(name, l):
                t = w[name]
                if isinstance(l, int):
                    return t[l]
                return t[bass.ds(l, 1)].rearrange("o p c -> (o p) c")

            def load_a(l):
                sp.dma_start(wqk[:, :], row("wqk", l)).then_inc(wa_loaded, 16)
                if full:
                    sp.dma_start(acols[:, :], row("acols", l)).then_inc(wa_loaded, 16)

            def load_v(l):
                sp.dma_start(wv[:, :], row("wv", l)).then_inc(wv_loaded, 16)
                if full:
                    sp.dma_start(bvb[:, :], row("bvb", l)).then_inc(wv_loaded, 16)

            def load_d(l):
                sp.dma_start(wo[:, :], row("wo", l)).then_inc(wd_loaded, 16)
                if full:
                    sp.dma_start(dcols[:, :], row("dcols", l)).then_inc(wd_loaded, 16)
                    sp.dma_start(w1[:, :], row("w1", l)).then_inc(wd_loaded, 16)
                    sp.dma_start(w2[:, :, :].rearrange("p f c -> p (f c)"), row("w2", l)).then_inc(wd_loaded, 16)

            def load_x(a, b):
                if full:
                    if needed((a.n - BATCH + 1) * 2):
                        at = count(sp, (a.n - BATCH + 1) * 2)
                        sp.wait_ge(ready, READY)
                        sp.wait_ge(ln_ready, at)
                if needed(a.value(1, 0)):
                    at = count(sp, a.value(1, 0))
                    sp.wait_ge(ready, READY)
                    sp.wait_ge(k_proj, at)
                if needed(a.value(1, 0)):
                    at = count(sp, a.value(1, 0))
                    sp.wait_ge(ready, READY)
                    sp.wait_ge(v_proj, at)
                sp.dma_start(xs[:, :], x_of(a)).then_inc(x_loaded, 16)

            def pack(a):
                at = count(sp, a.value(1, 1))
                sp.wait_ge(ready, READY)
                sp.wait_ge(q_lo, at)
                if needed(a.value(48, 0)):
                    at = count(sp, a.value(48, 0))
                    sp.wait_ge(ready, READY)
                    sp.wait_ge(heads_loaded, at)
                for r, n in enumerate(QROLES):
                    sp.dma_start(qpack[r:MAXROW:ROLES, :, :], qparts[:, n, :]).then_inc(q_packed, 16)
                at = count(sp, a.value(1, 1))
                sp.wait_ge(ready, READY)
                sp.wait_ge(k_lo, at)
                for r, n in enumerate(KROLES):
                    sp.dma_start(kpack[r:MAXROW:ROLES, :, :], kparts[:, n, :]).then_inc(k_packed, 16)

            def spread(b):
                at = count(sp, b.value(QD, QD))
                sp.wait_ge(ready, READY)
                sp.wait_ge(q_packed, at)
                at = count(sp, b.value(KD, KD))
                sp.wait_ge(ready, READY)
                sp.wait_ge(k_packed, at)
                if needed((b.n - 1) * PQ):
                    at = count(sp, (b.n - 1) * PQ)
                    sp.wait_ge(ready, READY)
                    sp.wait_ge(st_filled, at)
                sp.dma_start(keys[0:MAXROW, b.par, :, :], kpack[0:MAXROW, :, :]).then_inc(heads_loaded, 16)
                for j in range(2):
                    sp.dma_start(qz[ROWS * j:ROWS * (j + 1), b.par, j:HEADS:2, :],
                                 qpack[ROWS * j:ROWS * (j + 1), :, :]).then_inc(heads_loaded, 16)

            def load_max(u, half):
                H = HEADS // 2
                at = count(sp, u.value(2, half + 1))
                sp.wait_ge(ready, READY)
                sp.wait_ge(mrows_ready, at)
                sp.dma_start(qz[MAXROW:CONTRACT, u.par, H * half:H * (half + 1), :], mrows[:, :]).then_inc(max_loaded, 16)

            load_a(0)
            load_v(0)
            load_d(0)
            sp.wait_ge(ready, READY)

            def step(k, phase):
                a, b, c, d = stage_units(k, phase % 2)
                if b.there:
                    spread(b)
                if full and phase == 0 and a.there and not (isinstance(k, int) and k == 0):
                    if needed(a.value(2, 0)):
                        at = count(sp, a.value(2, 0))
                        sp.wait_ge(ready, READY)
                        sp.wait_ge(k_evac, at)
                    load_a(layer(a))
                if a.there:
                    load_x(a, b)
                if full and phase == 0 and a.there and not (isinstance(k, int) and k == 0):
                    if needed(a.value(1, 0)):
                        at = count(sp, a.value(1, 0))
                        sp.wait_ge(ready, READY)
                        sp.wait_ge(v_ready, at)
                    load_v(layer(a))
                if full and phase == 3 and d.there and not (isinstance(d.n, int) and d.n == 0):
                    if needed(d.value(2, 0)):
                        at = count(sp, d.value(2, 0))
                        sp.wait_ge(ready, READY)
                        sp.wait_ge(ln_ready, at)
                    load_d(layer(d))
                if c.there:
                    load_max(c, 1)
                if a.there:
                    pack(a)
                if b.there:
                    load_max(b, 0)

            if loop is None:
                for k in range(units + 3):
                    step(k, k % 4)
            else:
                for k in range(loop[0]):
                    step(k, k % 4)
                with sp.Fori(loop[0], loop[1], 4) as k:
                    for n in range(4):
                        step(k + n, n)
                for k in range(loop[1], units + 3):
                    step(k, k % 4)


def clear(nc, semaphores):
    with nc.Block() as block:
        @block.gpsimd
        def _(pool):
            for s in semaphores:
                pool.sem_clear(s)


def rows_phase(nc, env, name, src, rounds, dest, after=None):
    stream, rows = env["stream"], env["rows"]
    ident = env["ident"]
    with ExitStack() as ctx:
        def sb(n, shape, dt=F32):
            return ctx.enter_context(nc.sbuf_tensor(f"{name}_{n}", shape, dt))

        used = []

        def sem(n):
            used.append(ctx.enter_context(nc.semaphore(f"{name}_{n}")))
            return used[-1]

        turned_out = [ctx.enter_context(nc.psum_tensor(f"{name}_out{b}", [P, 512], F32)) for b in range(BATCH)]
        turned_in = [ctx.enter_context(nc.psum_tensor(f"{name}_in{b}", [P, 512], F32)) for b in range(BATCH)]
        stats, mv = sb("stats", [P, BATCH * TILES, 6]), sb("mv", [P, BATCH * TILES, 2])
        veps, rstd = sb("veps", [P, BATCH * TILES]), sb("rstd", [P, BATCH * TILES])
        minus_mean, offset = sb("minus_mean", [P, BATCH * TILES]), sb("offset", [P, BATCH * TILES])
        z = sb("z", [P, BATCH, TILES * P])
        src_turned, stats_ready, mv_ready = sem("src_turned"), sem("stats_ready"), sem("mv_ready")
        veps_ready, rstd_ready, scaled = sem("veps_ready"), sem("rstd_ready"), sem("scaled")
        mean_ready, offset_ready = sem("mean_ready"), sem("offset_ready")
        added, rows_turned, dest_ready, placed = sem("added"), sem("rows_turned"), sem("dest_ready"), sem("placed")
        stored = sem("stored")
        ctx.callback(lambda: clear(nc, used))
        block = ctx.enter_context(nc.Block())

        def tile(t, b, i):
            return t[:, b, i * P:(i + 1) * P]

        @block.tensor
        def _(pe):
            if src is not None:
                for b in range(BATCH):
                    for i in range(TILES):
                        mm = pe.transpose(turned_in[b][:, i * P:(i + 1) * P], tile(src, b, i), ident[:, :])
                    mm.then_inc(src_turned, 1)
            if dest is not None:
                for b in range(BATCH):
                    pe.wait_ge(scaled, (rounds - 1) * BATCH + b + 1)
                    for i in range(TILES):
                        mm = pe.transpose(turned_out[b][:, i * P:(i + 1) * P], tile(rows, b, i), ident[:, :])
                    mm.then_inc(rows_turned, 1)

        def data(r, b, i):
            if src is not None and r == 0:
                return turned_in[b][:, i * P:(i + 1) * P]
            return tile(rows if src is None and r > 0 else stream, b, i)

        @block.vector
        def _(dve):
            def statistics(r, b):
                for i in range(TILES):
                    bn = dve.bn_stats(stats[:, b * TILES + i, :], data(r, b, i))
                bn.then_inc(stats_ready, 1)
                dve.wait_ge(stats_ready, r * BATCH + b + 1)
                if r:
                    dve.wait_ge(offset_ready, (r - 1) * BATCH + b + 1)
                for i in range(TILES):
                    bn = dve.bn_aggr(mv[:, b * TILES + i, :], stats[:, b * TILES + i, :])
                bn.then_inc(mv_ready, 1)

            for b in range(BATCH):
                if src is not None:
                    dve.wait_ge(src_turned, b + 1)
                statistics(0, b)
            for b in range(BATCH):
                dve.wait_ge(scaled, b + 1)
                if src is not None:
                    dve.tensor_tensor(stream[:, b, :], stream[:, b, :], z[:, b, :], ALU.add).then_inc(added, 1)
                    if rounds > 1:
                        dve.wait_ge(added, b + 1)
                if rounds > 1:
                    statistics(1, b)
            if after == "positions":
                for b in range(BATCH):
                    dve.wait_ge(dest_ready, b + 1)
                    dve.tensor_tensor(dest(b), dest(b), env["positions"][:, :], ALU.add).then_inc(placed, 1)

        @block.gpsimd
        def _(pool):
            for r in range(rounds):
                for b in range(BATCH):
                    n = r * BATCH + b + 1
                    cut = slice(b * TILES, (b + 1) * TILES)
                    pool.wait_ge(mv_ready, n)
                    pool.tensor_scalar(veps[:, cut], mv[:, cut, 1], EPS, None, ALU.add).then_inc(veps_ready, 1)
                    pool.tensor_scalar(minus_mean[:, cut], mv[:, cut, 0], -1.0, None, ALU.mult).then_inc(mean_ready, 1)
                    pool.wait_ge(veps_ready, n)
                    if r:
                        pool.wait_ge(scaled, n - BATCH)
                    pool.tensor_tensor(rstd[:, cut], veps[:, cut], env["minus_half"][:, 0:TILES], ALU.pow
                                       ).then_inc(rstd_ready, 1)
                    pool.wait_ge(mean_ready, n)
                    pool.wait_ge(rstd_ready, n)
                    pool.tensor_tensor(offset[:, cut], minus_mean[:, cut], rstd[:, cut], ALU.mult
                                       ).then_inc(offset_ready, 1)

        @block.scalar
        def _(act):
            def place(b):
                act.wait_ge(rows_turned, b + 1)
                if after == "positions":
                    act.activation(dest(b), turned_out[b][:, :], ACT.Identity, bias=env["norm_in"][:, 1:2],
                                   scale=env["norm_in"][:, 0:1]).then_inc(dest_ready, 1)
                else:
                    act.copy(dest(b), turned_out[b][:, :]).then_inc(dest_ready, 1)

            for r in range(rounds):
                for b in range(BATCH):
                    act.wait_ge(offset_ready, r * BATCH + b + 1)
                    for i in range(TILES):
                        t = b * TILES + i
                        ts = act.activation(tile(z if src is not None and r == 0 else rows, b, i), data(r, b, i),
                                            ACT.Identity, bias=offset[:, t:t + 1], scale=rstd[:, t:t + 1])
                    ts.then_inc(scaled, 1)
                    if dest is not None and r == rounds - 1 and b:
                        place(b - 1)
            if dest is not None:
                place(BATCH - 1)

        @block.sync
        def _(sp):
            if dest is None:
                for b in range(BATCH):
                    sp.wait_ge(added, b + 1)
                    sp.dma_start(env["out_rows"][:, b * TILES:(b + 1) * TILES, :],
                                 stream[:, b, :].rearrange("p (i c) -> p i c", c=P)).then_inc(stored, 16)
                sp.wait_ge(stored, 16 * BATCH)


def mix_phase(nc, env, src, dest):
    with ExitStack() as ctx:
        def sb(n, shape, dt=F32):
            return ctx.enter_context(nc.sbuf_tensor(f"mix_{n}", shape, dt))

        used = []

        def sem(n):
            used.append(ctx.enter_context(nc.semaphore(f"mix_{n}")))
            return used[-1]

        banks = {n: [ctx.enter_context(nc.psum_tensor(f"mix_{n}{i}", [P, 512], F32)) for i in range(2)] for n in "rkv"}
        w, mu = env["mixw"], env["mu"]
        diff, xr, xk = sb("diff", [P, BATCH, SEQ]), sb("xr", [P, BATCH, SEQ]), sb("xk", [P, BATCH, SEQ])
        gate, kpos, ksq = sb("gate", [P, BATCH, SEQ]), sb("kpos", [P, BATCH, SEQ]), sb("ksq", [P, BATCH, SEQ])
        diffed, shifted = sem("diffed"), sem("shifted")
        r_proj, k_proj, v_proj = sem("r_proj"), sem("k_proj"), sem("v_proj")
        gated, positive, squared, mixed = sem("gated"), sem("positive"), sem("squared"), sem("mixed")
        ctx.callback(lambda: clear(nc, used))
        block = ctx.enter_context(nc.Block())

        @block.vector
        def _(dve):
            for b in range(BATCH):
                now, prev = src[:, b, 1:SEQ + 1], src[:, b, 0:SEQ]
                dve.tensor_tensor(diff[:, b, :], now, prev, ALU.subtract).then_inc(diffed, 1)
                dve.wait_ge(diffed, b + 1)
                dve.scalar_tensor_tensor(out=xr[:, b, :], in0=diff[:, b, :], scalar=mu[:, 0:1], in1=prev,
                                         op0=ALU.mult, op1=ALU.add).then_inc(shifted, 1)
                dve.scalar_tensor_tensor(out=xk[:, b, :], in0=diff[:, b, :], scalar=mu[:, 1:2], in1=prev,
                                         op0=ALU.mult, op1=ALU.add).then_inc(shifted, 1)
            for b in range(BATCH):
                dve.wait_ge(positive, b + 1)
                dve.tensor_tensor(ksq[:, b, :], kpos[:, b, :], kpos[:, b, :], ALU.mult).then_inc(squared, 1)
                dve.wait_ge(v_proj, b + 1)
                dve.wait_ge(gated, b + 1)
                dve.tensor_tensor(dest[:, b, :], banks["v"][b % 2][:, :], gate[:, b, :], ALU.mult).then_inc(mixed, 1)

        @block.tensor
        def _(pe):
            for b in range(BATCH + 1):
                if b < BATCH:
                    pe.wait_ge(shifted, 2 * b + 1)
                    if needed(b - 1):
                        pe.wait_ge(gated, b - 1)
                    pe.matmul(banks["r"][b % 2][:, :], w[:, 0:P], xr[:, b, :], start=True, stop=True).then_inc(r_proj, 1)
                    pe.wait_ge(shifted, 2 * b + 2)
                    if needed(b - 1):
                        pe.wait_ge(positive, b - 1)
                    pe.matmul(banks["k"][b % 2][:, :], w[:, P:2 * P], xk[:, b, :], start=True, stop=True
                              ).then_inc(k_proj, 1)
                if b >= 1:
                    if needed(b):
                        pe.wait_ge(squared, b)
                    if needed(b - 2):
                        pe.wait_ge(mixed, b - 2)
                    pe.matmul(banks["v"][(b - 1) % 2][:, :], w[:, 2 * P:3 * P], ksq[:, b - 1, :], start=True, stop=True
                              ).then_inc(v_proj, 1)

        @block.scalar
        def _(act):
            for b in range(BATCH):
                act.wait_ge(r_proj, b + 1)
                act.activation(gate[:, b, :], banks["r"][b % 2][:, :], ACT.Sigmoid).then_inc(gated, 1)
                act.wait_ge(k_proj, b + 1)
                act.activation(kpos[:, b, :], banks["k"][b % 2][:, :], ACT.Relu).then_inc(positive, 1)


def gate_phase(nc, env, src):
    import math
    N = BATCH * TILES
    with ExitStack() as ctx:
        def sb(n, shape, dt=F32):
            return ctx.enter_context(nc.sbuf_tensor(f"gate_{n}", shape, dt))

        used = []

        def sem(n):
            used.append(ctx.enter_context(nc.semaphore(f"gate_{n}")))
            return used[-1]

        ph_ps = ctx.enter_context(nc.psum_tensor("gate_bank", [P, 512], F32))
        wph, active_int = env["w_phase"], env["active_int"]
        heads = env["head_rows"]
        ph, size = sb("ph", [P, N, 2]), sb("size", [P, N, 2])
        big, zero, inv = sb("big", [P, N]), sb("zero", [P, N]), sb("inv", [P, N])
        sn, cs, s2, c2, r2, rinv = (sb(n, [P, N]) for n in ("sn", "cs", "s2", "c2", "r2", "rinv"))
        arg, turns, whole = sb("arg", [P, 2, HEADS]), sb("turns", [P, 2, HEADS]), sb("whole", [P, 2, HEADS], I32)
        wholef, trig = sb("wholef", [P, 2, HEADS]), sb("trig", [P, 2, HEADS])
        ibw, unlock = sb("ibw", [P, HEADS]), sb("unlock", [P, HEADS])
        t1, t2, win = sb("t1", [P, N, HEADS]), sb("t2", [P, N, HEADS]), sb("win", [P, N, HEADS])
        phased, done, r2_ready = sem("phased"), sem("done"), sem("r2_ready")
        rinv_ready, arg_ready, trig_ready = sem("rinv_ready"), sem("arg_ready"), sem("trig_ready")
        exponent_ready, window_ready = sem("exponent_ready"), sem("window_ready")
        gate = env["gate"]
        ctx.callback(lambda: clear(nc, used))
        block = ctx.enter_context(nc.Block())

        @block.tensor
        def _(pe):
            for b in range(BATCH):
                for i in range(TILES):
                    n = b * TILES + i
                    mm = pe.matmul(ph_ps[:, 2 * n:2 * n + 2], src[:, b, 1 + i * P:1 + (i + 1) * P], wph[:, :],
                                   start=True, stop=True)
            mm.then_inc(phased, 1)

        @block.scalar
        def _(act):
            act.wait_ge(arg_ready, 1)
            act.activation(trig[:, :, :], arg[:, :, :], ACT.Sin).then_inc(trig_ready, 1)
            act.wait_ge(exponent_ready, 1)
            act.activation(win[:, :, :], t1[:, :, :], ACT.Exp).then_inc(window_ready, 1)

        @block.gpsimd
        def _(pool):
            pool.wait_ge(r2_ready, 1)
            pool.tensor_tensor(rinv[:, :], r2[:, :], env["minus_half"][:, :], ALU.pow).then_inc(rinv_ready, 1)

        @block.vector
        def _(dve):
            links = [0]

            def link(ins):
                links[0] += 1
                ins.then_inc(done, 1)
                dve.wait_ge(done, links[0])

            def per_tile(t):
                return t[:, :].unsqueeze(2).to_broadcast([P, N, HEADS])

            def per_head(t):
                return t.unsqueeze(1).to_broadcast([P, N, HEADS])

            link(dve.tensor_copy(env["active"][:, :], active_int[:, :]))
            link(dve.tensor_copy(arg[:, 0, :], heads[:, 0, :]))
            link(dve.tensor_scalar(arg[:, 1, :], heads[:, 0, :], math.pi / 2, None, ALU.add))
            link(dve.tensor_scalar(turns[:, :, :], arg[:, :, :], 1 / (2 * math.pi), None, ALU.mult))
            link(dve.tensor_copy(whole[:, :, :], turns[:, :, :]))
            link(dve.tensor_copy(wholef[:, :, :], whole[:, :, :]))
            high = 6.28125
            for part in (high, 2 * math.pi - high):
                link(dve.scalar_tensor_tensor(out=arg[:, :, :], in0=wholef[:, :, :], scalar=-part, in1=arg[:, :, :],
                                              op0=ALU.mult, op1=ALU.add))
            dve.tensor_scalar(arg[:, :, :], arg[:, :, :], 3.1415925, -3.1415925, ALU.min, ALU.max).then_inc(arg_ready, 1)
            link(dve.reciprocal(ibw[:, :], heads[:, 2, :]))
            link(dve.tensor_scalar(unlock[:, :], heads[:, 1, :], -1.0, 1.0, ALU.mult, ALU.add))
            dve.wait_ge(phased, 1)
            link(dve.tensor_copy(ph[:, :, :], ph_ps[:, 0:2 * N].rearrange("p (n c) -> p n c", c=2)))
            link(dve.scalar_tensor_tensor(out=size[:, :, :], in0=ph[:, :, :], scalar=-1.0, in1=ph[:, :, :],
                                          op0=ALU.mult, op1=ALU.max))
            link(dve.tensor_tensor(big[:, :], size[:, :, 0], size[:, :, 1], ALU.max))
            link(dve.tensor_scalar(zero[:, :], big[:, :], 0.0, None, ALU.is_equal))
            link(dve.tensor_tensor(big[:, :], big[:, :], zero[:, :], ALU.add))
            link(dve.reciprocal(inv[:, :], big[:, :]))
            link(dve.tensor_tensor(sn[:, :], ph[:, :, 0], inv[:, :], ALU.mult))
            link(dve.tensor_tensor(cs[:, :], ph[:, :, 1], inv[:, :], ALU.mult))
            link(dve.tensor_tensor(cs[:, :], cs[:, :], zero[:, :], ALU.add))
            link(dve.tensor_tensor(s2[:, :], sn[:, :], sn[:, :], ALU.mult))
            link(dve.tensor_tensor(c2[:, :], cs[:, :], cs[:, :], ALU.mult))
            dve.tensor_tensor(r2[:, :], s2[:, :], c2[:, :], ALU.add).then_inc(r2_ready, 1)
            dve.wait_ge(rinv_ready, 1)
            link(dve.tensor_tensor(sn[:, :], sn[:, :], rinv[:, :], ALU.mult))
            link(dve.tensor_tensor(cs[:, :], cs[:, :], rinv[:, :], ALU.mult))
            dve.wait_ge(trig_ready, 1)
            link(dve.tensor_tensor(t1[:, :, :], per_tile(cs), per_head(trig[:, 1, :]), ALU.mult))
            link(dve.tensor_tensor(t2[:, :, :], per_tile(sn), per_head(trig[:, 0, :]), ALU.mult))
            link(dve.tensor_tensor(t1[:, :, :], t1[:, :, :], t2[:, :, :], ALU.add))
            dve.scalar_tensor_tensor(out=t1[:, :, :], in0=t1[:, :, :], scalar=-1.0, in1=per_head(ibw[:, :]),
                                     op0=ALU.add, op1=ALU.mult).then_inc(exponent_ready, 1)
            dve.wait_ge(window_ready, 1)
            link(dve.tensor_tensor(win[:, :, :], win[:, :, :], per_head(heads[:, 1, :]), ALU.mult))
            dve.scalar_tensor_tensor(out=gate[:, :, :], in0=win[:, :, :], scalar=LOG_EPS, in1=per_head(unlock[:, :]),
                                     op0=ALU.add, op1=ALU.add).then_inc(done, 1)


def experts_phase(nc, env, src, dest):
    with ExitStack() as ctx:
        def sb(n, shape, dt=F32):
            return ctx.enter_context(nc.sbuf_tensor(f"moe_{n}", shape, dt))

        used = []

        def sem(n):
            used.append(ctx.enter_context(nc.semaphore(f"moe_{n}")))
            return used[-1]

        jobs = [(b, r) for b in range(BATCH) for r in range(TOP)]
        hid_ps = [ctx.enter_context(nc.psum_tensor(f"moe_h{i}", [P, 512], F32)) for i in range(4)]
        z_ps = [ctx.enter_context(nc.psum_tensor(f"moe_z{i}", [P, 512], F32)) for i in range(2)]
        r_ps = ctx.enter_context(nc.psum_tensor("moe_r", [P, 512], F32))
        w1, w2, b1, b2, pick = (env[n] for n in ("rw1", "rw2", "rb1", "rb2", "pick"))
        wa, wb = sb("wa", [P, len(jobs), HIDDEN]), sb("wb", [P, len(jobs), CHUNKS, P])
        pooled, hr = sb("pooled", [P, BATCH]), sb("hr", [ROUTER, BATCH])
        logits, probs = sb("logits", [BATCH, EXPERTS]), sb("probs", [BATCH, EXPERTS])
        small = sb("small", [BATCH, 4])
        top, chosen, share = sb("top", [BATCH, 8]), sb("chosen", [BATCH, 8], U32), sb("share", [BATCH, 8])
        number = sb("number", [BATCH, 8], I32)
        weight = sb("weight", [P, BATCH, 8])
        hid = sb("hid", [P, 2, CHUNKS, SEQ])
        wa_loaded = [sem(f"wa_loaded{n}") for n in range(len(jobs))]
        wb_loaded = [sem(f"wb_loaded{n}") for n in range(len(jobs))]
        pooled_ready, hr_proj, hr_ready = sem("pooled_ready"), sem("hr_proj"), sem("hr_ready")
        logits_proj, shifted, exp_ready = sem("logits_proj"), sem("shifted"), sem("exp_ready")
        chosen_ready, share_ready, spread, done = sem("chosen_ready"), sem("share_ready"), sem("spread"), sem("done")
        hid_proj, hid_ready, z_proj, z_added = sem("hid_proj"), sem("hid_ready"), sem("z_proj"), sem("z_added")
        ctx.callback(lambda: clear(nc, used))
        block = ctx.enter_context(nc.Block())

        @block.sync
        def _(sp):
            d = env["dram"]
            sp.wait_ge(chosen_ready, 1)
            for n, (b, r) in enumerate(jobs):
                e = sp.value_load(number[b:b + 1, r:r + 1], min_val=0, max_val=EXPERTS - 1)
                sp.dma_start(wa[:, n, :], d["wa"][bass.ds(e, 1)].rearrange("o p c -> (o p) c")
                             ).then_inc(wa_loaded[n], 16)
                sp.dma_start(wb[:, n, :, :].rearrange("p f c -> p (f c)"),
                             d["wb"][bass.ds(e, 1)].rearrange("o p c -> (o p) c")).then_inc(wb_loaded[n], 16)

        @block.tensor
        def _(pe):
            pe.wait_ge(pooled_ready, 1)
            pe.matmul(r_ps[0:ROUTER, 0:BATCH], w1[:, :], pooled[:, :], start=True, stop=True).then_inc(hr_proj, 1)
            pe.wait_ge(hr_ready, 1)
            pe.matmul(r_ps[0:BATCH, 0:EXPERTS], hr[:, :], w2[:, :], start=True, stop=True).then_inc(logits_proj, 1)
            pe.wait_ge(share_ready, 1)
            for b in range(BATCH):
                mm = pe.matmul(r_ps[:, b * 8:(b + 1) * 8], pick[:, b, :], share[:, :], start=True, stop=True)
            mm.then_inc(spread, 1)

            for n in range(len(jobs) + 1):
                if n < len(jobs):
                    pe.wait_ge(wa_loaded[n], 16)
                    for f in range(CHUNKS):
                        if n >= 1:
                            pe.wait_ge(hid_ready, CHUNKS * (n - 1) + f + 1)
                        pe.matmul(hid_ps[f][:, :], wa[:, n, f * P:(f + 1) * P], src[:, jobs[n][0], 1:SEQ + 1],
                                  start=True, stop=True).then_inc(hid_proj, 1)
                if n >= 1:
                    pe.wait_ge(wb_loaded[n - 1], 16)
                    if n >= 3:
                        pe.wait_ge(z_added, n - 2)
                    for f in range(CHUNKS):
                        pe.wait_ge(hid_ready, CHUNKS * (n - 1) + f + 1)
                        mm = pe.matmul(z_ps[(n - 1) % 2][:, :], wb[:, n - 1, f, :], hid[:, (n - 1) % 2, f, :],
                                       start=(f == 0), stop=(f == CHUNKS - 1))
                    mm.then_inc(z_proj, 1)

        @block.scalar
        def _(act):
            act.wait_ge(hr_proj, 1)
            act.activation(hr[:, :], r_ps[0:ROUTER, 0:BATCH], ACT.Tanh, bias=b1[:, 0:1], scale=1.0 / SEQ
                           ).then_inc(hr_ready, 1)
            act.wait_ge(shifted, 1)
            act.activation(probs[:, :], logits[:, :], ACT.Exp, bias=small[:, 0:1], accum_out=small[:, 1:2]
                           ).then_inc(exp_ready, 1)
            for n in range(len(jobs)):
                if n >= 2:
                    act.wait_ge(z_proj, n - 1)
                for f in range(CHUNKS):
                    act.wait_ge(hid_proj, CHUNKS * n + f + 1)
                    act.activation(hid[:, n % 2, f, :], hid_ps[f][:, :], ACT.Gelu_apprx_tanh).then_inc(hid_ready, 1)

        @block.vector
        def _(dve):
            links = [0]

            def link(ins):
                links[0] += 1
                ins.then_inc(done, 1)
                dve.wait_ge(done, links[0])

            dve.tensor_reduce(pooled[:, :], src[:, :, 1:SEQ + 1], AX.X, ALU.add).then_inc(pooled_ready, 1)
            dve.wait_ge(logits_proj, 1)
            link(dve.tensor_tensor(logits[:, :], r_ps[0:BATCH, 0:EXPERTS], b2[:, :], ALU.add))
            dve.tensor_reduce(small[:, 0:1], logits[:, :], AX.X, ALU.max, negate=True).then_inc(shifted, 1)
            dve.wait_ge(exp_ready, 1)
            link(dve.reciprocal(small[:, 2:3], small[:, 1:2]))
            link(dve.tensor_scalar(probs[:, :], probs[:, :], small[:, 2:3], None, ALU.mult))
            link(dve.max(top[:, :], probs[:, :]))
            link(dve.max_index(chosen[:, :], top[:, :], probs[:, :]))
            dve.tensor_copy(number[:, :], chosen[:, :]).then_inc(chosen_ready, 1)
            link(dve.tensor_reduce(small[:, 3:4], top[:, 0:TOP], AX.X, ALU.add))
            link(dve.reciprocal(small[:, 3:4], small[:, 3:4]))
            dve.tensor_scalar(share[:, :], top[:, :], small[:, 3:4], None, ALU.mult).then_inc(share_ready, 1)
            dve.wait_ge(spread, 1)
            link(dve.tensor_copy(weight[:, :, :], r_ps[:, 0:BATCH * 8].rearrange("p (b e) -> p b e", e=8)))
            for n, (b, r) in enumerate(jobs):
                dve.wait_ge(z_proj, n + 1)
                if r:
                    dve.wait_ge(z_added, n)
                dve.scalar_tensor_tensor(out=dest[:, b, :], in0=z_ps[n % 2][:, :], scalar=weight[:, b, r:r + 1],
                                         in1=src[:, b, 1:SEQ + 1] if r == 0 else dest[:, b, :],
                                         op0=ALU.mult, op1=ALU.add).then_inc(z_added, 1)


def program(nc, dram, out):
    with ExitStack() as ctx:
        def sb(n, shape, dt=F32):
            return ctx.enter_context(nc.sbuf_tensor(n, shape, dt))

        env = {"dram": dram, "out_rows": out.rearrange("(n p) c -> p n c", p=P)}
        ident, identb = sb("ident", [P, P]), sb("identb", [P, P], BF16)
        stream = sb("stream", [P, BATCH, TILES * P])
        rows = sb("rows", [P, BATCH, TILES * P])
        feats = sb("feats", [P, BATCH, SEQ + 1])
        made = sb("made", [P, BATCH, SEQ])
        positions = sb("positions", [P, SEQ])
        norm_in, last_row = sb("norm_in", [P, 2]), sb("last_row", [P, 1])
        minus_half = sb("minus_half", [P, BATCH * TILES])
        window_mask, causal_mask = sb("window_mask", [P, 2 * P]), sb("causal_mask", [P, SEQ])
        gate, active = sb("gate", [P, BATCH * TILES, HEADS]), sb("active", [P, HEADS])
        mixw, mu = sb("mixw", [P, 3 * P]), sb("mu", [P, 2])
        w_phase, head_rows, active_int = sb("w_phase", [P, 2]), sb("head_rows", [P, 3, HEADS]), sb("active_int", [P, HEADS], I32)
        rw1, rw2 = sb("rw1", [P, ROUTER]), sb("rw2", [ROUTER, EXPERTS])
        rb1, rb2, pick = sb("rb1", [ROUTER, 1]), sb("rb2", [BATCH, EXPERTS]), sb("pick", [BATCH, BATCH, P])
        later = dict(mixw=mixw, mu=mu, w_phase=w_phase, head_rows=head_rows, active_int=active_int,
                     rw1=rw1, rw2=rw2, rb1=rb1, rb2=rb2, pick=pick)
        env.update(later)
        env.update(ident=ident, identb=identb, stream=stream, rows=rows, positions=positions, norm_in=norm_in,
                   last_row=last_row, minus_half=minus_half, gate=gate, active=active)

        with ExitStack() as first:
            loaded = first.enter_context(nc.semaphore("loaded"))
            set_up = first.enter_context(nc.semaphore("set_up"))
            first.callback(lambda: clear(nc, [loaded, set_up]))
            with nc.Block() as block:
                @block.sync
                def _(sp):
                    sp.dma_start(stream[:, :, :].rearrange("p b (i c) -> p (b i) c", c=P),
                                 dram["x"].rearrange("(n p) c -> p n c", p=P)).then_inc(loaded, 16)
                    for t, n in ((ident, "ident"), (positions, "positions"), (norm_in, "norm_in"),
                                 (last_row, "last_row"), (window_mask, "window_mask"), (causal_mask, "causal_mask")):
                        sp.dma_start(t[:, :], dram[n]).then_inc(loaded, 16)
                    for n, t in later.items():
                        sp.dma_start(t[:], dram[n]).then_inc(loaded, 16)
                    sp.wait_ge(loaded, (7 + len(later)) * 16)

                @block.vector
                def _(dve):
                    dve.memset(minus_half[:, :], -0.5).then_inc(set_up, 1)
                    dve.memset(feats[:, :, 0:1], 0.0).then_inc(set_up, 1)
                    dve.wait_ge(loaded, (7 + len(later)) * 16)
                    dve.tensor_copy(identb[:, :], ident[:, :]).then_inc(set_up, 1)

        state = made
        rows_phase(nc, env, "prepare", None, 2, lambda b: state[:, b, :], "positions")
        env.update(state=state, source=state, result=state, mask=window_mask,
                   weights={n: dram[n] for n in ("wqk", "acols", "wv", "bvb", "wo", "dcols", "w1", "w2")})
        attention(nc, env, Windowed, True, LAYERS * BATCH, (4, LAYERS * BATCH))
        rows_phase(nc, env, "after_layers", state, 2, lambda b: feats[:, b, 1:SEQ + 1])
        mix_phase(nc, env, feats, made)
        rows_phase(nc, env, "after_mix", made, 2, lambda b: feats[:, b, 1:SEQ + 1])
        gate_phase(nc, env, feats)
        env.update(state=None, source=feats[:, :, 1:SEQ + 1], result=made, mask=causal_mask,
                   weights={n: dram["c" + n] for n in ("wqk", "wv", "wo")})
        attention(nc, env, Causal, False, BATCH, None)
        rows_phase(nc, env, "after_attention", made, 2, lambda b: feats[:, b, 1:SEQ + 1])
        experts_phase(nc, env, feats, made)
        rows_phase(nc, env, "after_experts", made, 1, None)


def lay_out(v):
    import numpy as np

    def T(a):
        return np.swapaxes(a, -1, -2)

    L = LAYERS
    perm = np.arange(P).reshape(PAIRS, 2, HEAD).transpose(1, 2, 0).reshape(P)
    wqkv, bqkv = v["L0_attn_Wqkv"], v["L0_attn_bqkv"]
    half = P // 2
    phase = np.arange(SEQ, dtype=np.float32)[:, None] / (
        np.float32(10000.0) ** (np.arange(half, dtype=np.float32) / np.float32(half - 1)))[None, :]
    q = np.arange(P)[:, None]
    c = np.arange(2 * P)[None, :]
    k = np.arange(SEQ)[None, :] - (SEQ - P)
    d = {
        "x": v["L0_attn_x"].reshape(BATCH * SEQ, P),
        "ident": np.eye(P, dtype=np.float32),
        "positions": T(np.concatenate([np.cos(phase), np.sin(phase)], axis=-1)).astype(np.float32),
        "norm_in": np.stack([v["L0_attn_norm_in_g"], v["L0_attn_norm_in_b"]], axis=1),
        "last_row": (np.arange(P) == P - 1).astype(np.float32)[:, None],
        "window_mask": np.where((c >= q + P - WINDOW) & (c <= q + P), 0.0, NEG).astype(np.float32),
        "causal_mask": np.where(k <= q, 0.0, NEG).astype(np.float32),
        "wqk": np.concatenate([T(wqkv[:, :P])[..., perm], T(wqkv[:, P:2 * P])[..., perm]], axis=-1),
        "wv": T(wqkv[:, 2 * P:]),
        "acols": np.stack([bqkv[:, :P][:, perm], bqkv[:, P:2 * P][:, perm]], axis=2),
        "bvb": np.broadcast_to(bqkv[:, None, 2 * P:], (L, P, P)),
        "wo": T(v["L0_attn_Wo"]),
        "w1": T(v["L0_attn_W1"]),
        "w2": T(v["L0_attn_W2"]).reshape(L, CHUNKS, P, P).transpose(0, 2, 1, 3).reshape(L, P, CHUNKS * P),
        "dcols": np.concatenate([np.stack([v["L0_attn_" + n] for n in ("bo", "ln1_g", "ln1_b", "ln2_g", "ln2_b", "b2")],
                                          axis=2), v["L0_attn_b1"].reshape(L, CHUNKS, P).transpose(0, 2, 1)], axis=2),
        "mixw": np.concatenate([T(v["L0_ffn_W_" + n]) for n in "rkv"], axis=1),
        "mu": np.stack([v["L0_ffn_mu_r"], v["L0_ffn_mu_k"]], axis=1),
        "cwqk": np.concatenate([v["L1_attn_wq"][:, perm], v["L1_attn_wk"][:, perm]], axis=1)[None],
        "cwv": v["L1_attn_wv"][None],
        "cwo": v["L1_attn_wo"][None],
        "w_phase": v["L1_attn_w_phase"],
        "head_rows": np.broadcast_to(np.stack([v["L1_attn_carrier"], v["L1_attn_lock"], v["L1_attn_bandwidth"]])[None],
                                     (P, 3, HEADS)),
        "active_int": np.broadcast_to(v["L1_attn_active_mask"].astype(np.int32)[None], (P, HEADS)),
        "rw1": v["L1_ffn_W1"],
        "rw2": v["L1_ffn_W2"],
        "rb1": v["L1_ffn_b1"][:, None],
        "rb2": np.broadcast_to(v["L1_ffn_b2"][None], (BATCH, EXPERTS)),
        "pick": np.repeat(np.eye(BATCH, dtype=np.float32)[:, :, None], P, axis=2),
        "wa": v["L1_ffn_Wa"],
        "wb": v["L1_ffn_Wb"].reshape(EXPERTS, CHUNKS, P, P).transpose(0, 2, 1, 3).reshape(EXPERTS, P, CHUNKS * P),
    }
    return {n: np.ascontiguousarray(a) for n, a in d.items()}


def kernel(**inputs):
    import numpy as _np
    import concourse.bacc as _bacc
    from concourse import mybir as _mybir
    from concourse.bass_utils import run_bass_kernel_spmd as _run

    nc = _bacc.Bacc("TRN2", target_bir_lowering=False, num_devices=1)
    arrays, dram = {}, {}
    for name, a in lay_out({n: _np.asarray(a) for n, a in inputs.items()}).items():
        arrays[f"in_{name}"] = a
        dram[name] = nc.dram_tensor(f"in_{name}", a.shape, _mybir.dt.from_np(a.dtype), kind="ExternalInput").ap()
    out = nc.dram_tensor("out", (BATCH * SEQ, P), F32, kind="ExternalOutput").ap()
    program(nc, dram, out)
    r = _run(nc, [arrays], core_ids=[0])
    return r.results[0]["out"].reshape(BATCH, SEQ, P)
```
